# Optimizing a Trainium2 kernel written in Bass

```python
import numpy as np
import jax
import jax.numpy as jnp

def _softmax(x, axis=-1):
    return jax.nn.softmax(x, axis=axis)

def _gelu(x):
    return jax.nn.gelu(x, approximate=True)

def _silu(x):
    return jax.nn.silu(x)

def _sigmoid(x):
    return jax.nn.sigmoid(x)

def _layernorm(x, axis=-1, eps=1e-05):
    m = jnp.mean(x, axis=axis, keepdims=True)
    v = jnp.var(x, axis=axis, keepdims=True)
    return (x - m) / jnp.sqrt(v + eps)

def _scatter_add(tgt, idx, src, axis=0):
    return tgt.at[idx].add(src)

def _segment_sum(src, seg, n):
    return jax.ops.segment_sum(src, seg, n)
kernel_name = 'mk_macaron_d1_jaxref_r8_2b5938'

def setup_inputs(seed: int=0):
    np.random.seed(seed)
    _w = jnp.asarray

    def _L0_attn_setup():
        import jax, jax.numpy as jnp
        import numpy as np
        N_HEADS = 16
        CHUNK = 128

        def _phi(x):
            return jax.nn.elu(x) + 1.0
        key = jax.random.key(seed)
        ks = jax.random.split(key, 5)
        d = 128
        scale = (2.0 / (d + d)) ** 0.5
        W = lambda k: jax.random.normal(k, (d, d), jnp.float32) * scale
        return {'x': jax.random.normal(ks[0], (4, 512, d), jnp.float32), 'Wq': W(ks[1]), 'bq': jnp.zeros((d,), jnp.float32), 'Wk': W(ks[2]), 'bk': jnp.zeros((d,), jnp.float32), 'Wv': W(ks[3]), 'bv': jnp.zeros((d,), jnp.float32), 'Wo': W(ks[4]), 'bo': jnp.zeros((d,), jnp.float32)}
    _L0_attn_in = _L0_attn_setup()

    def _L0_ffn_setup():
        import jax, jax.numpy as jnp
        import numpy as np
        EPS = float(jnp.finfo(jnp.float32).eps)
        TOP_K = 2

        def rmsnorm(x, w):
            return x * jax.lax.rsqrt(jnp.mean(x * x, axis=-1, keepdims=True) + EPS) * w
        B, T, D_IN, D_MODEL, D_FF, D_OUT, E = (8, 128, 128, 128, 512, 128, 8)
        STD = 0.02
        key = jax.random.key(seed)
        ks = jax.random.split(key, 8)
        return {'s': jax.random.normal(ks[0], (B, T, D_IN), dtype=jnp.float32), 'W_in': STD * jax.random.normal(ks[1], (D_MODEL, D_IN), dtype=jnp.float32), 'in_norm_w': jnp.ones((D_MODEL,), dtype=jnp.float32), 'Wr': STD * jax.random.normal(ks[2], (E, D_MODEL), dtype=jnp.float32), 'expert_bias': jnp.zeros((E,), dtype=jnp.float32), 'Wg': STD * jax.random.normal(ks[3], (E, D_FF, D_MODEL), dtype=jnp.float32), 'Wu': STD * jax.random.normal(ks[4], (E, D_FF, D_MODEL), dtype=jnp.float32), 'Wd': STD * jax.random.normal(ks[5], (E, D_MODEL, D_FF), dtype=jnp.float32), 'enorm_w': jnp.ones((E, D_MODEL), dtype=jnp.float32), 'out_norm_w': jnp.ones((D_MODEL,), dtype=jnp.float32), 'W_out': STD * jax.random.normal(ks[6], (D_OUT, D_MODEL), dtype=jnp.float32)}
    _L0_ffn_in = _L0_ffn_setup()
    _d = {'L0_attn_x': _L0_attn_in['x'], 'L0_attn_Wq': _L0_attn_in['Wq'], 'L0_attn_bq': _L0_attn_in['bq'], 'L0_attn_Wk': _L0_attn_in['Wk'], 'L0_attn_bk': _L0_attn_in['bk'], 'L0_attn_Wv': _L0_attn_in['Wv'], 'L0_attn_bv': _L0_attn_in['bv'], 'L0_attn_Wo': _L0_attn_in['Wo'], 'L0_attn_bo': _L0_attn_in['bo'], 'L0_ffn_W_in': _L0_ffn_in['W_in'], 'L0_ffn_in_norm_w': _L0_ffn_in['in_norm_w'], 'L0_ffn_Wr': _L0_ffn_in['Wr'], 'L0_ffn_expert_bias': _L0_ffn_in['expert_bias'], 'L0_ffn_Wg': _L0_ffn_in['Wg'], 'L0_ffn_Wu': _L0_ffn_in['Wu'], 'L0_ffn_Wd': _L0_ffn_in['Wd'], 'L0_ffn_enorm_w': _L0_ffn_in['enorm_w'], 'L0_ffn_out_norm_w': _L0_ffn_in['out_norm_w'], 'L0_ffn_W_out': _L0_ffn_in['W_out']}
    _x0 = _d['L0_attn_x']
    _d['L0_attn_x'] = jax.random.normal(jax.random.fold_in(jax.random.key(seed), 1), (8, 1024, 128), dtype=_x0.dtype)
    del _x0
    return _d

def reference(L0_attn_x, L0_attn_Wq, L0_attn_bq, L0_attn_Wk, L0_attn_bk, L0_attn_Wv, L0_attn_bv, L0_attn_Wo, L0_attn_bo, L0_ffn_W_in, L0_ffn_in_norm_w, L0_ffn_Wr, L0_ffn_expert_bias, L0_ffn_Wg, L0_ffn_Wu, L0_ffn_Wd, L0_ffn_enorm_w, L0_ffn_out_norm_w, L0_ffn_W_out):

    def _L0_attn_ref(x, Wq, bq, Wk, bk, Wv, bv, Wo, bo):
        import jax, jax.numpy as jnp
        import numpy as np
        N_HEADS = 16
        CHUNK = 128

        def _phi(x):
            return jax.nn.elu(x) + 1.0
        b, s, dm = x.shape
        h = N_HEADS
        d = dm // h

        def proj(W, bias):
            y = x @ W.T + bias
            return y.reshape(b, s, h, d).transpose(0, 2, 1, 3).reshape(b * h, s, d)
        q = _phi(proj(Wq, bq))
        k = _phi(proj(Wk, bk))
        v = proj(Wv, bv)
        C = CHUNK
        n = s // C
        to_chunks = lambda t: t.reshape(b * h, n, C, d).transpose(1, 0, 2, 3)
        qc, kc, vc = (to_chunks(q), to_chunks(k), to_chunks(v))
        mask = jnp.tril(jnp.ones((C, C), bool))

        def step(carry, inp):
            S, z = carry
            qi, ki, vi = inp
            scores = jnp.einsum('bqd,bkd->bqk', qi, ki)
            scores = jnp.where(mask, scores, jnp.zeros((), scores.dtype))
            num = jnp.einsum('bqk,bkd->bqd', scores, vi) + jnp.einsum('bqd,bde->bqe', qi, S)
            kcum = jnp.cumsum(ki, axis=1) + z[:, None, :]
            den = jnp.sum(qi * kcum, axis=-1, keepdims=True)
            out = num / den
            S2 = S + jnp.einsum('bkd,bke->bde', ki, vi)
            z2 = z + ki.sum(axis=1)
            return ((S2, z2), out)
        init = (jnp.zeros((b * h, d, d), x.dtype), jnp.zeros((b * h, d), x.dtype))
        _, outs = jax.lax.scan(step, init, (qc, kc, vc))
        out = outs.transpose(1, 0, 2, 3).reshape(b, h, s, d).transpose(0, 2, 1, 3).reshape(b, s, dm)
        return out @ Wo.T + bo

    def _L0_ffn_ref(s, W_in, in_norm_w, Wr, expert_bias, Wg, Wu, Wd, enorm_w, out_norm_w, W_out):
        import jax, jax.numpy as jnp
        import numpy as np
        EPS = float(jnp.finfo(jnp.float32).eps)
        TOP_K = 2

        def rmsnorm(x, w):
            return x * jax.lax.rsqrt(jnp.mean(x * x, axis=-1, keepdims=True) + EPS) * w
        B, T, _ = s.shape
        x = s.reshape(B * T, -1)
        h = rmsnorm(x @ W_in.T, in_norm_w)
        logits = h @ Wr.T
        _, idx = jax.lax.top_k(logits + expert_bias, TOP_K)
        sel = jnp.take_along_axis(logits, idx, axis=-1)
        g_topk = jax.nn.softmax(sel, axis=-1)
        N = logits.shape[0]
        gates = jnp.zeros_like(logits).at[jnp.arange(N)[:, None], idx].set(g_topk)
        out = jnp.zeros_like(h)
        for e in range(Wg.shape[0]):
            gate = jax.nn.silu(h @ Wg[e].T)
            up = h @ Wu[e].T
            oe = rmsnorm(gate * up @ Wd[e].T, enorm_w[e])
            out = out + gates[:, e:e + 1] * oe
        s_hat = rmsnorm(out, out_norm_w) @ W_out.T
        return s_hat.reshape(B, T, -1)
    x = L0_attn_x
    x = x + 0.5 * _L0_ffn_ref(_layernorm(x, axis=-1), L0_ffn_W_in, L0_ffn_in_norm_w, L0_ffn_Wr, L0_ffn_expert_bias, L0_ffn_Wg, L0_ffn_Wu, L0_ffn_Wd, L0_ffn_enorm_w, L0_ffn_out_norm_w, L0_ffn_W_out)
    x = x + _L0_attn_ref(_layernorm(x, axis=-1), L0_attn_Wq, L0_attn_bq, L0_attn_Wk, L0_attn_bk, L0_attn_Wv, L0_attn_bv, L0_attn_Wo, L0_attn_bo)
    x = x + 0.5 * _L0_ffn_ref(_layernorm(x, axis=-1), L0_ffn_W_in, L0_ffn_in_norm_w, L0_ffn_Wr, L0_ffn_expert_bias, L0_ffn_Wg, L0_ffn_Wu, L0_ffn_Wd, L0_ffn_enorm_w, L0_ffn_out_norm_w, L0_ffn_W_out)
    return x

_drawn_inputs = setup_inputs


def setup_inputs(seed=0):
    import zlib

    import numpy as np

    out = dict(_drawn_inputs(seed))
    spreads = {'L0_attn_bq': (0.0, 0.1),
     'L0_attn_bk': (0.0, 0.1),
     'L0_attn_bv': (0.0, 0.1),
     'L0_attn_bo': (0.0, 0.1),
     'L0_ffn_in_norm_w': (1.0, 0.2),
     'L0_ffn_expert_bias': (0.0, 0.1),
     'L0_ffn_enorm_w': (1.0, 0.2),
     'L0_ffn_out_norm_w': (1.0, 0.2)}
    factors = {}
    for name, (base, spread) in spreads.items():
        noise = np.random.default_rng([zlib.crc32(name.encode()), seed]).standard_normal(out[name].shape)
        drawn = base * np.exp(spread * noise) if base else spread * noise
        out[name] = jnp.asarray(drawn.astype(out[name].dtype))
    for name, factor in factors.items():
        out[name] = (out[name] * factor).astype(out[name].dtype)
    return out
```

```python
from contextlib import ExitStack

import concourse.bass as bass
import concourse.mybir as mybir
import numpy as np

F32, BF16, I32 = mybir.dt.float32, mybir.dt.bfloat16, mybir.dt.int32
ALU, ACT, AX = mybir.AluOpType, mybir.ActivationFunctionType, mybir.AxisListType

P = 128
BATCH, SEQ = 8, 1024
TILES = BATCH * SEQ // P
FIRST = 2
QUAD = 4
GROUPS = TILES // QUAD
EXPERTS, TOP, FF = 8, 2, 512
CHUNKS = FF // P
SLOT_TILES = TILES * TOP + EXPERTS
HEADS, HD = 16, 8
HV = HD + 1
CHUNK_TILES = SEQ // P
KV = HEADS * HV * HD
LN_EPS = 1e-5
RMS_EPS = float(np.finfo(np.float32).eps)
ROW = P + 4
BACK = 4
OUT_ROWS = TOP * TILES * P
SCATTER_LAG = 7


def wait(engine, semaphore, value):
    if not isinstance(value, int) or value > 0:
        engine.wait_ge(semaphore, value)


def wait_apart(engine, semaphore, value, passed):
    engine.wait_ge(semaphore, value)
    engine.sem_inc(passed, 1)


THIRDS = [(0, 6 * HV * HD), (6 * HV * HD, 11 * HV * HD), (11 * HV * HD, KV)]


def least(a, b):
    return a if not isinstance(a, int) else min(a, b)


def staggered(engine, count, unroll, steps, before=None, back=2):
    most = max(lag for lag, _ in steps)
    depth = -(-(most + back) // unroll) * unroll

    def turn(base, k):
        for lag, fn in steps:
            i = base + k - lag
            if not isinstance(i, int) or 0 <= i < count:
                fn(i, (k - lag) % unroll)

    for t in range(depth):
        if before and t % unroll == 0:
            before(t)
        turn(t - t % unroll, t % unroll)
    with engine.Fori(depth // unroll, count // unroll) as body:
        t = body * unroll
        if before:
            before(t)
        for k in range(unroll):
            turn(t, k)
    for t in range(count, count + most):
        if before and t % unroll == 0:
            before(t)
        turn(t - t % unroll, t % unroll)


def build(nc, d):
    with ExitStack() as ctx:
        def sb(name, shape, dt=F32):
            return ctx.enter_context(nc.sbuf_tensor(name, shape, dt))

        def sem(name):
            return ctx.enter_context(nc.semaphore(name))

        x = sb("x", [P, TILES, P])
        w_in, w_out, wo = sb("w_in", [P, P]), sb("w_out", [P, P]), sb("w_o", [P, P])
        wr = sb("w_router", [P, EXPERTS])
        wqkv = sb("w_qkv", [P, 3 * P])
        wg, wu = sb("w_gate", [P, EXPERTS * FF]), sb("w_up", [P, EXPERTS * FF])
        wd = sb("w_down", [P, EXPERTS * FF])
        in_norm, out_norm = sb("in_norm", [P, 1]), sb("out_norm", [P, 1])
        enorm = sb("enorm", [P, EXPERTS * P])
        rbias = sb("router_bias", [P, EXPERTS])
        bqkv, bo = sb("b_qkv", [P, 3 * P]), sb("b_o", [P, P])
        ident, upto_here, before_here = sb("ident", [P, P]), sb("upto_here", [P, P]), sb("before_here", [P, P])
        ones = sb("ones", [P, P])
        head_mask = sb("head_mask", [P, HEADS * HV])
        iota_col = sb("iota_col", [P, SLOT_TILES])
        iota_bf = sb("iota_bf", [P, SLOT_TILES], BF16)
        pair_row = sb("pair_row", [P, TOP * TILES])
        spare_row = sb("spare_row", [P, SLOT_TILES])
        eps_ln, eps_rms = sb("eps_ln", [P, 1]), sb("eps_rms", [P, 1])

        logits = sb("logits", [P, TILES, EXPERTS])
        gates = sb("gates", [P, TILES, EXPERTS])
        picked = sb("picked", [P, TILES, EXPERTS])
        slot_of = sb("slot_of", [P, TILES, EXPERTS])
        scratch = sb("route_scratch", [P, TILES, EXPERTS])
        wide = sb("wide", [P, BACK * TOP * QUAD * ROW])
        beats = wide[:, 0:TILES * EXPERTS * EXPERTS].rearrange("p (t a b) -> p t a b", a=EXPERTS, b=EXPERTS)
        over = wide[:, 0:EXPERTS * TILES].rearrange("p (e t) -> p e t", e=EXPERTS)
        ended = wide[:, 0:EXPERTS * SLOT_TILES].rearrange("p (t e) -> p t e", e=EXPERTS)
        read = wide[:, 0:2 * KV].rearrange("p (u n) -> p u n", u=2)
        back = wide[:, :].rearrange("p (b w k r) -> p b w k r", b=BACK, w=TOP, k=QUAD)
        per_token = sb("per_token", [P, 2, TILES])
        pair_gate = sb("pair_gate", [P, TOP, TILES])
        pair_slot = sb("pair_slot", [P, TOP, TILES])
        pair_int = sb("pair_int", [P, 2, TOP, TILES], I32)
        pair_tile, pair_place = sb("pair_tile", [P, TOP, TILES]), sb("pair_place", [P, TOP, TILES])
        picks_here = sb("picks_here", [P, EXPERTS])
        counts = sb("counts", [P, EXPERTS])
        tile_count, tile_end = sb("tile_count", [P, EXPERTS]), sb("tile_end", [P, EXPERTS])
        first_slot = sb("first_slot", [P, EXPERTS])
        hot_place, hot_row = sb("hot_place", [P, 4, P]), sb("hot_row", [P, 4, SLOT_TILES])
        row_of, row_tmp = sb("row_of", [P, SLOT_TILES]), sb("row_tmp", [P, SLOT_TILES])
        gather_row = sb("gather_row", [P, SLOT_TILES], I32)
        scatter_row = sb("scatter_row", [P, SLOT_TILES], I32)
        tile_expert = sb("tile_expert", [P, SLOT_TILES + 8], I32)

        stats = sb("stats", [P, 2, QUAD, 6])
        mean_var = sb("mean_var", [P, 2, QUAD, 2])
        std, rstd = sb("std", [P, 2, QUAD]), sb("rstd", [P, 2, QUAD])
        ln = sb("ln", [P, 2, QUAD, P])
        ln_t = sb("ln_t", [P, 2, QUAD * P])
        squares = sb("squares", [P, 2, QUAD, P])
        scaled_lo = sb("scaled_lo", [P, 2, QUAD, P])
        sumsq, rms, rrms = sb("sumsq", [P, 2, QUAD]), sb("rms", [P, 2, QUAD]), sb("rrms", [P, 2, QUAD])
        h = sb("h", [P, 2, QUAD, P])
        h_t = sb("h_t", [P, 2, QUAD * P])
        back_rms, back_scale = sb("back_rms", [P, 2, TOP, QUAD]), sb("back_scale", [P, 2, TOP, QUAD])

        gather_now, scatter_now = sb("gather_now", [P, 4], I32), sb("scatter_now", [P, 4], I32)
        slot_h = sb("slot_h", [P, 4, P])
        slot_ht = sb("slot_ht", [P, 2, P])
        silu = sb("silu", [P, 2, FF])
        act = sb("act", [P, 2, FF])
        act_t = sb("act_t", [P, 2, FF])
        slot_sq = sb("slot_sq", [P, 4, P])
        slot_out = sb("slot_out", [P, 4, ROW])

        qk = sb("qk", [P, 2, 2 * P])
        exps, relus = sb("exps", [P, 2, 2 * P]), sb("relus", [P, 2, 2 * P])
        phi = sb("phi", [P, 4, 2 * P])
        v_one = sb("v_one", [P, 4, HEADS * HV])
        kv = sb("kv", [P, 2, KV])
        intra = sb("intra", [P, 2, HEADS * HV])
        q_t = sb("q_t", [P, 4, P])
        state = sb("state", [P, 4, HEADS * HV])
        recip_den = sb("recip_den", [P, 2, HEADS])
        att = sb("att", [P, 2, P])
        att_t = sb("att_t", [P, 2, P])

        psum = ctx.enter_context(nc.psum_tensor("psum", [P, 8, 512], F32))
        h_dram = nc.dram_tensor("h_dram", [TILES * P, P], F32, kind="Internal").ap()
        out_dram = nc.dram_tensor("out_dram", [OUT_ROWS + SLOT_TILES * P, ROW], F32, kind="Internal").ap()

        loaded, first_loaded, rest_loaded, experts_loaded = sem("loaded"), sem("first_loaded"), sem("rest_loaded"), sem("experts_loaded")
        stage_done, passed = sem("stage_done"), sem("passed")
        x_tok = d["x"].rearrange("(t p) m -> p t m", p=P)
        out_tok = d["out"].rearrange("(t p) m -> p t m", p=P)

        bn_done, stats_done, std_ready, rstd_done = sem("bn_done"), sem("stats_done"), sem("std_ready"), sem("rstd_done")
        normed, ln_turned, ln_t_ready, h_product = sem("normed"), sem("ln_turned"), sem("ln_t_ready"), sem("h_product")
        sumsq_done, rms_ready, rrms_done, h_scaled = sem("sumsq_done"), sem("rms_ready"), sem("rrms_done"), sem("h_scaled")
        h_stored = [sem("h_stored0"), sem("h_stored1")]
        h_turned, h_t_ready, logits_done, logits_kept = sem("h_turned"), sem("h_t_ready"), sem("logits_done"), sem("logits_kept")
        route_step, route_act, route_exp, route_pe = sem("route_step"), sem("route_act"), sem("route_exp"), sem("route_pe")
        hot_ready, hot_used, rows_ready = sem("hot_ready"), sem("hot_used"), sem("rows_ready")
        gathered = [sem(f"gathered{k}") for k in range(4)]
        scattered = [sem(f"scattered{k}") for k in range(4)]
        gather_indexed, scatter_indexed = sem("gather_indexed"), sem("scatter_indexed")
        slot_turned, slot_ht_ready, gate_up = sem("slot_turned"), sem("slot_ht_ready"), sem("gate_up")
        silu_done, act_done, act_turned, act_t_ready = sem("silu_done"), sem("act_done"), sem("act_turned"), sem("act_t_ready")
        down_done, slot_sumsq, slot_ready = sem("down_done"), sem("slot_sumsq"), sem("slot_ready")
        back_loaded = [sem(f"back_loaded{k}") for k in range(BACK)]
        back_rms_ready, back_step, mixed = sem("back_rms_ready"), sem("back_step"), sem("mixed")
        mix_sumsq, mix_rms_ready, mix_rrms, mix_scaled = sem("mix_sumsq"), sem("mix_rms_ready"), sem("mix_rrms"), sem("mix_scaled")
        mix_turned, mix_t_ready, y_done, x_added, x_stored = sem("mix_turned"), sem("mix_t_ready"), sem("y_done"), sem("x_added"), sem("x_stored")
        a_bn, a_stats, a_std, a_rstd, a_normed = sem("a_bn"), sem("a_stats"), sem("a_std"), sem("a_rstd"), sem("a_normed")
        a_turned, a_ln_t, qkv_done, qkv_biased = sem("a_turned"), sem("a_ln_t"), sem("qkv_done"), sem("qkv_biased")
        a_exps, phi_ready, kv_ready, bo_added = sem("a_exps"), sem("phi_ready"), sem("kv_ready"), sem("bo_added")
        sums_done, read_done, reduced, q_turned, q_t_ready = sem("sums_done"), sem("read_done"), sem("reduced"), sem("q_turned"), sem("q_t_ready")
        state_done, state_ready, inter_done, total_done = sem("state_done"), sem("state_ready"), sem("inter_done"), sem("total_done")
        den_done, att_ready, att_turned, att_t_ready, o_done, att_added = (
            sem("den_done"), sem("att_ready"), sem("att_turned"), sem("att_t_ready"), sem("o_done"), sem("att_added"))
        ones_set = sem("ones_set")

        block = ctx.enter_context(nc.Block())

        def end_stage(engine, stage):
            engine.drain().then_inc(stage_done, 1)
            engine.wait_ge(stage_done, 5 * stage)

        SMALL_LOADS = [(w_in, "w_in"), (w_out, "w_out"), (wo, "wo"), (wr, "wr"), (wqkv, "wqkv"),
                       (in_norm, "in_norm"), (out_norm, "out_norm"), (ident, "ident"),
                       (upto_here, "upto_here"), (before_here, "before_here"), (head_mask, "head_mask"),
                       (iota_col, "iota_col"), (pair_row, "pair_row"),
                       (spare_row, "spare_row")]
        ROW_LOADS = [(enorm, "enorm"), (rbias, "rbias"), (bqkv, "bqkv"), (bo, "bo")]
        N_LOADS = len(SMALL_LOADS) + len(ROW_LOADS)

        @block.sync
        def _(sp):
            sp.dma_start(x[:, 0:QUAD * FIRST, :], x_tok[:, 0:QUAD * FIRST, :]).then_inc(first_loaded, 16)
            for dst, name in SMALL_LOADS:
                sp.dma_start(dst[:, :], d[name]).then_inc(loaded, 16)
            for dst, name in ROW_LOADS:
                sp.dma_start(dst[:, :], d[name].partition_broadcast(P)).then_inc(loaded, 16)
            sp.dma_start(x[:, QUAD * FIRST:TILES, :], x_tok[:, QUAD * FIRST:TILES, :]).then_inc(rest_loaded, 16)
            for dst, name in ((wg, "wg"), (wu, "wu"), (wd, "wd")):
                sp.dma_start(dst[:, :], d[name]).then_inc(experts_loaded, 16)
            end_stage(sp, 1)

            def ffn(layer, stage):
                off = layer * GROUPS

                def store_h(i, u):
                    sp.wait_ge(h_scaled, off + i + 1)
                    sp.dma_start(h_dram[bass.ds(i * (QUAD * P), QUAD * P), :].rearrange("(k p) m -> p k m", p=P),
                                 h[:, u, :, :]).then_inc(h_stored[u], 16)

                staggered(sp, GROUPS, 2, [(0, store_h)])
                for p in range(2):
                    sp.wait_ge(h_stored[p], 8 * (off + GROUPS))
                end_stage(sp, stage)
                end_stage(sp, stage + 1)
                end_stage(sp, stage + 2)

                def load_back(i, u):
                    wait(sp, mixed, off + i - 3)
                    for w in range(TOP):
                        rows = out_dram[bass.ds((i * QUAD + w * TILES) * P, QUAD * P), :]
                        sp.dma_start(back[:, u, w, :, :], rows.rearrange("(k p) m -> p k m", p=P)
                                     ).then_inc(back_loaded[u], 16)

                def store_x(i, u):
                    sp.wait_ge(x_added, off + i + 1)
                    sp.dma_start(out_tok[:, bass.ds(i * QUAD, QUAD), :], x[:, bass.ds(i * QUAD, QUAD), :]).then_inc(x_stored, 16)

                if layer == 0:
                    staggered(sp, GROUPS, BACK, [(0, load_back)], back=4)
                else:
                    staggered(sp, GROUPS, BACK, [(0, load_back), (5, store_x)], back=4)
                end_stage(sp, stage + 3)

            ffn(0, 2)
            end_stage(sp, 6)
            ffn(1, 7)
            sp.wait_ge(x_stored, 16 * GROUPS)

        @block.tensor
        def _(pe):
            end_stage(pe, 1)

            def ffn(layer, stage):
                off = layer * GROUPS

                def turn_ln(i, u):
                    pe.wait_ge(normed, off + i + 1)
                    wait(pe, ln_t_ready, off + i - 1)
                    for k in range(QUAD):
                        last = pe.transpose(psum[:, u, k * P:(k + 1) * P], ln[:, u, k, :], ident[:, :])
                    last.then_inc(ln_turned, 1)

                def product_in(i, u):
                    pe.wait_ge(ln_t_ready, off + i + 1)
                    wait(pe, h_scaled, off + i - 1)
                    for k in range(QUAD):
                        last = pe.matmul(psum[:, 2 + u, k * P:(k + 1) * P], ln_t[:, u, k * P:(k + 1) * P], w_in[:, :],
                                         start=True, stop=True)
                    last.then_inc(h_product, 1)

                def turn_h(i, u):
                    pe.wait_ge(h_scaled, off + i + 1)
                    wait(pe, h_t_ready, off + i - 1)
                    for k in range(QUAD):
                        last = pe.transpose(psum[:, 4 + u, k * P:(k + 1) * P], h[:, u, k, :], ident[:, :])
                    last.then_inc(h_turned, 1)

                def router(i, u):
                    pe.wait_ge(h_t_ready, off + i + 1)
                    wait(pe, logits_kept, off + i - 1)
                    for k in range(QUAD):
                        last = pe.matmul(psum[:, 6 + u, k * EXPERTS:(k + 1) * EXPERTS], h_t[:, u, k * P:(k + 1) * P],
                                         wr[:, :], start=True, stop=True)
                    last.then_inc(logits_done, 1)

                staggered(pe, GROUPS, 2, [(3, product_in), (2, turn_ln), (5, turn_h), (6, router)])
                end_stage(pe, stage)

                pe.wait_ge(route_pe, layer * 2 + 1)
                pe.matmul(psum[:, 0, 0:EXPERTS], before_here[:, :], picks_here[:, :], start=True, stop=True)
                pe.matmul(psum[:, 1, 0:EXPERTS], ones[:, :], picks_here[:, :], start=True, stop=True).then_inc(route_act, 1)

                def place(i, u):
                    pe.wait_ge(hot_ready, layer * TOP * TILES + i + 1)
                    pe.matmul(psum[:, 2, 0:SLOT_TILES], hot_place[:, u, :], hot_row[:, u, :],
                              start=False, stop=False, skip_group_check=True).then_inc(hot_used, 1)

                pe.wait_ge(route_pe, layer * 2 + 2)
                pe.matmul(psum[:, 2, 0:SLOT_TILES], hot_place[:, 0, :], hot_row[:, 0, :],
                          start=True, stop=False, skip_group_check=True).then_inc(route_act, 1)
                staggered(pe, TOP * TILES, 4, [(0, place)])
                end_stage(pe, stage + 1)

                pe.wait_ge(experts_loaded, 48)
                experts_off = layer * SLOT_TILES
                registers = [pe.alloc_register(f"expert_{layer}_{k}") for k in range(6)]
                weights_at = {}

                def read_experts(t):
                    pe.load(registers, tile_expert[0:1, bass.ds(t, 6)])
                    for k in range(6):
                        weights_at[k] = pe.snap(registers[k], min_val=0, max_val=(EXPERTS - 1) * P)

                def turn_slots(i, u):
                    pe.wait_ge(gathered[u], 4 * (experts_off + i) - 4 * u + 16)
                    wait(pe, slot_ht_ready, experts_off + i)
                    pe.transpose(psum[:, 0, 0:P], slot_h[:, u, :], ident[:, :]).then_inc(slot_turned, 1)

                def gate_and_up(i, u):
                    pe.wait_ge(slot_ht_ready, experts_off + i + 1)
                    wait(pe, act_done, experts_off + i - 1)
                    at = weights_at[(u + 1) % 4 + 2]
                    pe.matmul(psum[:, 1 + u % 2, :], slot_ht[:, u % 2, :], wg[:, bass.ds(at * CHUNKS, FF)], start=True, stop=True)
                    pe.matmul(psum[:, 3 + u % 2, :], slot_ht[:, u % 2, :], wu[:, bass.ds(at * CHUNKS, FF)],
                              start=True, stop=True).then_inc(gate_up, 1)

                def turn_act(i, u):
                    pe.wait_ge(act_done, experts_off + i + 1)
                    wait(pe, act_t_ready, experts_off + i - 1)
                    for c in range(CHUNKS):
                        last = pe.transpose(psum[:, 5 + u % 2, c * P:(c + 1) * P], act[:, u % 2, c * P:(c + 1) * P], ident[:, :])
                    last.then_inc(act_turned, 1)

                def down(i, u):
                    pe.wait_ge(act_t_ready, experts_off + i + 1)
                    wait(pe, slot_ready, experts_off + i)
                    at = weights_at[(u + 3) % 4]
                    for c in range(CHUNKS):
                        last = pe.matmul(psum[:, 7, 0:P], act_t[:, u % 2, c * P:(c + 1) * P], wd[:, bass.ds(at * CHUNKS + c * P, P)],
                                         start=(c == 0), stop=(c == CHUNKS - 1))
                    last.then_inc(down_done, 1)

                staggered(pe, SLOT_TILES, 4, [(1, gate_and_up), (0, turn_slots), (2, turn_act), (3, down)], before=read_experts)
                end_stage(pe, stage + 2)

                def turn_mix(i, u):
                    pe.wait_ge(mix_scaled, off + i + 1)
                    wait(pe, mix_t_ready, off + i - 1)
                    for k in range(QUAD):
                        last = pe.transpose(psum[:, u, k * P:(k + 1) * P], h[:, u, k, :], ident[:, :])
                    last.then_inc(mix_turned, 1)

                def product_out(i, u):
                    pe.wait_ge(mix_t_ready, off + i + 1)
                    wait(pe, x_added, off + i - 1)
                    for k in range(QUAD):
                        last = pe.matmul(psum[:, 2 + u, k * P:(k + 1) * P], h_t[:, u, k * P:(k + 1) * P], w_out[:, :],
                                         start=True, stop=True)
                    last.then_inc(y_done, 1)

                staggered(pe, GROUPS, 2, [(5, product_out), (4, turn_mix)])
                end_stage(pe, stage + 3)

            def attention():
                def turn_ln(i, u):
                    if u % QUAD == 0:
                        q = u // QUAD
                        pe.wait_ge(a_normed, i + QUAD)
                        wait(pe, a_ln_t, i)
                        wait(pe, att_added, i - 9)
                        for k in range(QUAD):
                            last = pe.transpose(psum[:, 0, k * P:(k + 1) * P], ln[:, q, k, :], ident[:, :])
                        last.then_inc(a_turned, QUAD)

                def product_qkv(i, u):
                    q, k = u // QUAD, u % QUAD
                    pe.wait_ge(a_ln_t, i - k + QUAD)
                    wait(pe, qkv_biased, i)
                    pe.matmul(psum[:, 1, 0:3 * P], ln_t[:, q, k * P:(k + 1) * P], wqkv[:, :], start=True, stop=True).then_inc(qkv_done, 1)

                def turn_q(i, u):
                    pe.wait_ge(phi_ready, i + 1)
                    wait(pe, q_t_ready, i)
                    wait(pe, att_t_ready, i - 4)
                    pe.transpose(psum[:, 6, 0:P], phi[:, u % 4, 0:P], ident[:, :]).then_inc(q_turned, 1)

                def add_state(i, u):
                    wait(pe, state_ready, i)
                    pe.wait_ge(phi_ready, i + 1)
                    pe.matmul(psum[:, 5, 0:HEADS * HV], phi[:, u % 4, P:2 * P], v_one[:, u % 4, :],
                              start=(u == 0), stop=(u == CHUNK_TILES - 1), skip_group_check=True).then_inc(state_done, 1)

                def sums(i, u):
                    pe.wait_ge(kv_ready, i + 1)
                    for n, (a, b) in enumerate(THIRDS):
                        wait(pe, read_done, 3 * i + n - 2)
                        pe.matmul(psum[:, 2 + n, 0:b - a], upto_here[:, :], kv[:, u % 2, a:b], start=True, stop=True).then_inc(sums_done, 1)

                def read_state(i, u):
                    pe.wait_ge(q_t_ready, i + 1)
                    wait(pe, state_ready, i)
                    wait(pe, total_done, i)
                    pe.matmul(psum[:, 7, 0:HEADS * HV], q_t[:, u % 4, :], state[:, (u + 3) % 4, :], start=True, stop=True).then_inc(inter_done, 1)

                def turn_att(i, u):
                    pe.wait_ge(att_ready, i + 1)
                    wait(pe, att_t_ready, i)
                    wait(pe, q_t_ready, least(i + 5, TILES))
                    pe.transpose(psum[:, 6, 0:P], att[:, u % 2, :], ident[:, :]).then_inc(att_turned, 1)

                def product_o(i, u):
                    pe.wait_ge(att_t_ready, i + 1)
                    wait(pe, att_added, i)
                    wait(pe, a_ln_t, least(i + 13 - (u + 1) % QUAD, TILES))
                    pe.matmul(psum[:, 0, 0:P], att_t[:, u % 2, :], wo[:, :], start=True, stop=True).then_inc(o_done, 1)

                staggered(pe, TILES, CHUNK_TILES, [(7, turn_q), (7, add_state), (4, product_qkv), (8, sums), (9, read_state),
                                                   (3, turn_ln), (11, turn_att), (12, product_o)])
                end_stage(pe, 6)

            ffn(0, 2)
            attention()
            ffn(1, 7)

        @block.scalar
        def _(act_e):
            end_stage(act_e, 1)

            def ffn(layer, stage):
                off = layer * GROUPS

                def root_variance(i, u):
                    act_e.wait_ge(stats_done, off + i + 1)
                    wait(act_e, normed, off + i - 1)
                    act_e.activation(std[:, u, :], mean_var[:, u, :, 1], ACT.Sqrt, bias=eps_ln[:, 0:1]).then_inc(std_ready, 1)

                def keep_ln_t(i, u):
                    act_e.wait_ge(ln_turned, off + i + 1)
                    wait(act_e, h_product, off + i - 1)
                    act_e.activation(ln_t[:, u, :], psum[:, u, :], ACT.Copy).then_inc(ln_t_ready, 1)

                def square_h(i, u):
                    act_e.wait_ge(h_product, off + i + 1)
                    wait(act_e, h_scaled, off + i - 1)
                    for k in range(QUAD):
                        last = act_e.activation(squares[:, u, k, :], psum[:, 2 + u, k * P:(k + 1) * P], ACT.Square,
                                                accum_out=sumsq[:, u, k:k + 1])
                    last.then_inc(sumsq_done, 1)
                    act_e.wait_ge(sumsq_done, off + i + 1)
                    act_e.activation(rms[:, u, :], sumsq[:, u, :], ACT.Sqrt, scale=1.0 / P, bias=eps_rms[:, 0:1]).then_inc(rms_ready, 1)

                def keep_h_t(i, u):
                    act_e.wait_ge(h_turned, off + i + 1)
                    wait(act_e, logits_done, off + i - 1)
                    act_e.activation(h_t[:, u, :], psum[:, 4 + u, :], ACT.Copy, scale=in_norm[:, 0:1]).then_inc(h_t_ready, 1)

                staggered(act_e, GROUPS, 2, [(3, square_h), (2, keep_ln_t), (5, keep_h_t), (0, root_variance)])
                end_stage(act_e, stage)

                act_e.wait_ge(route_exp, 2 * layer + 1)
                act_e.activation(gates[:, :, :], scratch[:, :, :], ACT.Exp).then_inc(route_exp, 1)
                end_stage(act_e, stage + 1)

                n0 = layer * SLOT_TILES

                def keep_slot_ht(i, u):
                    act_e.wait_ge(slot_turned, n0 + i + 1)
                    wait(act_e, gate_up, n0 + i - 1)
                    act_e.activation(slot_ht[:, u % 2, :], psum[:, 0, 0:P], ACT.Copy, scale=in_norm[:, 0:1]).then_inc(slot_ht_ready, 1)

                def silu_gate(i, u):
                    act_e.wait_ge(gate_up, n0 + i + 1)
                    wait(act_e, act_done, n0 + i - 1)
                    act_e.activation(silu[:, u % 2, :], psum[:, 1 + u % 2, :], ACT.Silu).then_inc(silu_done, 1)

                def keep_act_t(i, u):
                    act_e.wait_ge(act_turned, n0 + i + 1)
                    wait(act_e, down_done, n0 + i - 1)
                    act_e.activation(act_t[:, u % 2, :], psum[:, 5 + u % 2, :], ACT.Copy).then_inc(act_t_ready, 1)

                def square_slots(i, u):
                    act_e.wait_ge(down_done, n0 + i + 1)
                    wait(act_e, scattered[u], 4 * (n0 + i) - 4 * u)
                    act_e.activation(slot_sq[:, u, :], psum[:, 7, 0:P], ACT.Square,
                                     accum_out=slot_out[:, u, P:P + 1]).then_inc(slot_sumsq, 1)

                staggered(act_e, SLOT_TILES, 4, [(1, silu_gate), (0, keep_slot_ht), (2, keep_act_t), (3, square_slots)], back=4)
                end_stage(act_e, stage + 2)

                def root_back(i, u):
                    act_e.wait_ge(back_loaded[u], 8 * (off + i + BACK) - 8 * u)
                    wait(act_e, mixed, off + i - 1)
                    act_e.activation(back_rms[:, u % 2, :, :], back[:, u, :, :, P], ACT.Sqrt, scale=1.0 / P,
                                     bias=eps_rms[:, 0:1]).then_inc(back_rms_ready, 1)

                def square_mix(i, u):
                    act_e.wait_ge(mixed, off + i + 1)
                    wait(act_e, mix_rrms, off + i - 1)
                    for k in range(QUAD):
                        last = act_e.activation(squares[:, u % 2, k, :], ln[:, u % 2, k, :], ACT.Square,
                                                accum_out=sumsq[:, u % 2, k:k + 1])
                    last.then_inc(mix_sumsq, 1)
                    act_e.wait_ge(mix_sumsq, off + i + 1)
                    act_e.activation(rms[:, u % 2, :], sumsq[:, u % 2, :], ACT.Sqrt, scale=1.0 / P, bias=eps_rms[:, 0:1]).then_inc(mix_rms_ready, 1)

                def keep_mix_t(i, u):
                    act_e.wait_ge(mix_turned, off + i + 1)
                    wait(act_e, y_done, off + i - 1)
                    act_e.activation(h_t[:, u % 2, :], psum[:, u % 2, :], ACT.Copy, scale=out_norm[:, 0:1]).then_inc(mix_t_ready, 1)

                staggered(act_e, GROUPS, BACK, [(2, square_mix), (0, root_back), (4, keep_mix_t)])
                end_stage(act_e, stage + 3)

            def attention():
                def root_variance(i, u):
                    if u % QUAD == 0:
                        q = u // QUAD
                        act_e.wait_ge(a_stats, i + QUAD)
                        wait(act_e, a_normed, i - QUAD)
                        act_e.activation(std[:, q, :], mean_var[:, q, :, 1], ACT.Sqrt, bias=eps_ln[:, 0:1]).then_inc(a_std, QUAD)

                def keep_ln_t(i, u):
                    if u % QUAD == 0:
                        q = u // QUAD
                        act_e.wait_ge(a_turned, i + QUAD)
                        wait(act_e, qkv_done, i - QUAD)
                        act_e.activation(ln_t[:, q, :], psum[:, 0, :], ACT.Copy).then_inc(a_ln_t, QUAD)

                def elu_parts(i, u):
                    act_e.wait_ge(qkv_biased, i + 1)
                    wait(act_e, phi_ready, i - 1)
                    act_e.activation(exps[:, u % 2, :], qk[:, u % 2, :], ACT.Exp)
                    act_e.activation(relus[:, u % 2, :], qk[:, u % 2, :], ACT.Relu).then_inc(a_exps, 1)

                def keep_q_t(i, u):
                    act_e.wait_ge(q_turned, i + 1)
                    wait(act_e, inter_done, i - 3)
                    act_e.activation(q_t[:, u % 4, :], psum[:, 6, 0:P], ACT.Copy).then_inc(q_t_ready, 1)

                def keep_att_t(i, u):
                    act_e.wait_ge(att_turned, i + 1)
                    wait(act_e, o_done, i - 1)
                    act_e.activation(att_t[:, u % 2, :], psum[:, 6, 0:P], ACT.Copy).then_inc(att_t_ready, 1)

                staggered(act_e, TILES, CHUNK_TILES, [(7, keep_q_t), (5, elu_parts), (3, keep_ln_t), (11, keep_att_t), (1, root_variance)])
                end_stage(act_e, 6)

            ffn(0, 2)
            attention()
            ffn(1, 7)

        @block.gpsimd
        def _(pool):
            pool.memset(slot_out[:, :, :], 0.0)
            end_stage(pool, 1)

            def ffn(layer, stage):
                end_stage(pool, stage)
                end_stage(pool, stage + 1)
                n0 = layer * SLOT_TILES

                def gather(i, u):
                    wait(pool, slot_turned, n0 + i - 3)
                    pool.tensor_copy(gather_now[:, u:u + 1], gather_row[:, bass.ds(i, 1)]).then_inc(gather_indexed, 1)
                    wait_apart(pool, gather_indexed, n0 + i + 1, passed)
                    pool.indirect_dma_start(out=slot_h[:, u, :], out_offset=None, in_=h_dram[:, :],
                                            in_offset=bass.IndirectOffsetOnAxis(ap=gather_now[:, u:u + 1], axis=0)
                                            ).then_inc(gathered[u], 16)

                def scatter(i, u):
                    pool.wait_ge(slot_ready, n0 + i + 1)
                    pool.tensor_copy(scatter_now[:, u:u + 1], scatter_row[:, bass.ds(i, 1)]).then_inc(scatter_indexed, 1)
                    wait_apart(pool, scatter_indexed, n0 + i + 1, passed)
                    pool.indirect_dma_start(out=out_dram[:, :],
                                            out_offset=bass.IndirectOffsetOnAxis(ap=scatter_now[:, u:u + 1], axis=0),
                                            in_=slot_out[:, u, :], in_offset=None).then_inc(scattered[u], 16)

                staggered(pool, SLOT_TILES, 4, [(0, gather), (SCATTER_LAG, scatter)])
                for u in range(4):
                    pool.wait_ge(scattered[u], 4 * (n0 + SLOT_TILES))
                end_stage(pool, stage + 2)
                end_stage(pool, stage + 3)

            def attention():
                def products(i, u):
                    pool.wait_ge(phi_ready, i + 1)
                    wait(pool, sums_done, 3 * i - 3)
                    k = phi[:, u % 4, P:2 * P].rearrange("p (h d) -> p h d", h=HEADS)
                    v = v_one[:, u % 4, :].rearrange("p (h e) -> p h e", h=HEADS)
                    pool.tensor_tensor(kv[:, u % 2, :].rearrange("p (h e d) -> p h e d", h=HEADS, e=HV),
                                       k.unsqueeze(2).broadcast_to([P, HEADS, HV, HD]),
                                       v.unsqueeze(3).broadcast_to([P, HEADS, HV, HD]), ALU.mult).then_inc(kv_ready, 1)

                def add_bo(i, u):
                    pool.wait_ge(a_normed, i + 1)
                    xt = x[:, bass.ds(i, 1), :].rearrange("p a m -> p (a m)")
                    pool.tensor_tensor(xt, xt, bo[:, :], ALU.add).then_inc(bo_added, 1)

                staggered(pool, TILES, CHUNK_TILES, [(7, products), (7, add_bo)])
                end_stage(pool, 6)

            ffn(0, 2)
            attention()
            ffn(1, 7)

        @block.vector
        def _(dve):
            step = [0]
            dve.memset(ones[:, :], 1.0)
            dve.memset(v_one[:, :, :], 1.0)
            dve.memset(state[:, :, :], 0.0)
            dve.memset(tile_expert[:, :], 0)
            dve.memset(eps_ln[:, :], LN_EPS)
            dve.memset(eps_rms[:, :], RMS_EPS).then_inc(ones_set, 1)
            dve.wait_ge(loaded, 16 * N_LOADS)
            dve.tensor_copy(iota_bf[:, :], iota_col[:, :])
            end_stage(dve, 1)

            def ffn(layer, stage):
                off = layer * GROUPS

                def statistics(i, u):
                    if layer == 0 and isinstance(i, int) and i in (0, FIRST):
                        dve.wait_ge(first_loaded if i == 0 else rest_loaded, 16)
                    wait(dve, std_ready, off + i - 1)
                    for k in range(QUAD):
                        last = dve.bn_stats(stats[:, u, k, :], x[:, bass.ds(i * QUAD + k, 1), :].rearrange("p a m -> p (a m)"))
                    last.then_inc(bn_done, 1)
                    wait_apart(dve, bn_done, off + i + 1, passed)
                    for k in range(QUAD):
                        last = dve.bn_aggr(mean_var[:, u, k, :], stats[:, u, k, :])
                    last.then_inc(stats_done, 1)

                def normalise(i, u):
                    dve.wait_ge(std_ready, off + i + 1)
                    dve.reciprocal(rstd[:, u, :], std[:, u, :]).then_inc(rstd_done, 1)
                    wait(dve, ln_turned, off + i - 1)
                    dve.wait_ge(rstd_done, off + i + 1)
                    for k in range(QUAD):
                        last = dve.tensor_scalar(ln[:, u, k, :], x[:, bass.ds(i * QUAD + k, 1), :].rearrange("p a m -> p (a m)"),
                                                 mean_var[:, u, k, 0:1], rstd[:, u, k:k + 1], ALU.subtract, ALU.mult)
                    last.then_inc(normed, 1)

                def scale_h(i, u):
                    dve.wait_ge(rms_ready, off + i + 1)
                    dve.reciprocal(rrms[:, u, :], rms[:, u, :]).then_inc(rrms_done, 1)
                    wait(dve, h_turned, off + i - 1)
                    wait(dve, h_stored[u], 8 * (off + i) - 8 * u)
                    dve.wait_ge(rrms_done, off + i + 1)
                    dve.tensor_tensor(h[:, u, :, :], psum[:, 2 + u, :].rearrange("p (k m) -> p k m", m=P),
                                      rrms[:, u, :].unsqueeze(2).broadcast_to([P, QUAD, P]), ALU.mult).then_inc(h_scaled, 1)

                def keep_logits(i, u):
                    dve.wait_ge(logits_done, off + i + 1)
                    dve.tensor_copy(logits[:, bass.ds(i * QUAD, QUAD), :].rearrange("p k e -> p (k e)"),
                                    psum[:, 6 + u, 0:QUAD * EXPERTS]).then_inc(logits_kept, 1)

                staggered(dve, GROUPS, 2, [(4, scale_h), (1, normalise), (0, statistics), (7, keep_logits)])
                end_stage(dve, stage)


                def then(instruction):
                    step[0] += 1
                    instruction.then_inc(route_step, 1)
                    dve.wait_ge(route_step, step[0])

                def over_experts(ap):
                    return ap.unsqueeze(2).broadcast_to([P, TILES, EXPERTS])

                def over_tiles(ap):
                    return ap.unsqueeze(1).broadcast_to([P, TILES, EXPERTS])

                then(dve.tensor_tensor(scratch[:, :, :], logits[:, :, :], over_tiles(rbias[:, :]), ALU.add))
                diagonal = wide[:, 0:TILES * EXPERTS * EXPERTS].rearrange("p (t n) -> p t n", t=TILES)[:, :, 0:EXPERTS * EXPERTS:EXPERTS + 1]
                then(dve.memset(diagonal, 0.0))
                for e in range(EXPERTS):
                    if e:
                        last = dve.tensor_tensor(beats[:, :, e, 0:e], scratch[:, :, 0:e],
                                                 scratch[:, :, e:e + 1].broadcast_to([P, TILES, e]), ALU.is_ge)
                    if e < EXPERTS - 1:
                        n = EXPERTS - 1 - e
                        last = dve.tensor_tensor(beats[:, :, e, e + 1:EXPERTS], scratch[:, :, e + 1:EXPERTS],
                                                 scratch[:, :, e:e + 1].broadcast_to([P, TILES, n]), ALU.is_gt)
                then(last)
                then(dve.tensor_reduce(slot_of[:, :, :], beats[:, :, :, :], AX.X, ALU.add))
                then(dve.tensor_scalar(picked[:, :, :], slot_of[:, :, :], float(TOP) - 0.5, None, ALU.is_lt))
                then(dve.tensor_scalar(scratch[:, :, :], picked[:, :, :], -1.0, 1e30, ALU.add, ALU.mult))
                then(dve.tensor_tensor(scratch[:, :, :], scratch[:, :, :], logits[:, :, :], ALU.add))
                then(dve.tensor_reduce(per_token[:, 0, :], scratch[:, :, :], AX.X, ALU.max))
                dve.tensor_tensor(scratch[:, :, :], scratch[:, :, :], over_experts(per_token[:, 0, :]),
                                  ALU.subtract).then_inc(route_exp, 1)
                dve.tensor_reduce(picks_here[:, :], picked[:, :, :].rearrange("p t e -> p e t"), AX.X, ALU.add).then_inc(route_pe, 1)
                dve.wait_ge(route_exp, 2 * layer + 2)
                then(dve.tensor_reduce(per_token[:, 0, :], gates[:, :, :], AX.X, ALU.add))
                then(dve.reciprocal(per_token[:, 1, :], per_token[:, 0, :]))
                then(dve.tensor_tensor(gates[:, :, :], gates[:, :, :], over_experts(per_token[:, 1, :]), ALU.mult))
                dve.wait_ge(route_act, 2 * layer + 1)
                then(dve.tensor_copy(counts[:, :], psum[:, 1, 0:EXPERTS]))
                then(dve.tensor_scalar(row_tmp[:, 0:TILES], iota_col[:, 0:TILES], float(P), None, ALU.mult))
                then(dve.tensor_tensor(over, counts[:, :].unsqueeze(2).broadcast_to([P, EXPERTS, TILES]),
                                       row_tmp[:, 0:TILES].unsqueeze(1).broadcast_to([P, EXPERTS, TILES]), ALU.is_gt))
                then(dve.tensor_reduce(tile_count[:, :], over, AX.X, ALU.add))
                then(dve.tensor_tensor_scan(tile_end[:, :], ones[:, 0:EXPERTS], tile_count[:, :], 0.0, ALU.mult, ALU.add))
                then(dve.tensor_tensor(first_slot[:, :], tile_end[:, :], tile_count[:, :], ALU.subtract))
                then(dve.scalar_tensor_tensor(out=first_slot[:, :], in0=first_slot[:, :], scalar=float(P),
                                              in1=psum[:, 0, 0:EXPERTS], op0=ALU.mult, op1=ALU.add))
                for e in range(EXPERTS):
                    last = dve.tensor_tensor_scan(slot_of[:, :, e], ones[:, 0:TILES], picked[:, :, e],
                                                  first_slot[:, e:e + 1], ALU.mult, ALU.add)
                then(last)
                then(dve.tensor_tensor(slot_of[:, :, :], slot_of[:, :, :], picked[:, :, :], ALU.subtract))
                then(dve.tensor_tensor(slot_of[:, :, :], slot_of[:, :, :], picked[:, :, :], ALU.mult))
                then(dve.tensor_reduce(pair_slot[:, 1, :], slot_of[:, :, :], AX.X, ALU.max))
                then(dve.tensor_reduce(per_token[:, 0, :], slot_of[:, :, :], AX.X, ALU.add))
                then(dve.tensor_tensor(pair_slot[:, 0, :], per_token[:, 0, :], pair_slot[:, 1, :], ALU.subtract))
                then(dve.tensor_tensor(scratch[:, :, :], slot_of[:, :, :], over_experts(pair_slot[:, 1, :]), ALU.is_equal))
                then(dve.tensor_tensor(scratch[:, :, :], scratch[:, :, :], gates[:, :, :], ALU.mult))
                then(dve.tensor_reduce(pair_gate[:, 1, :], scratch[:, :, :], AX.X, ALU.add))
                then(dve.tensor_tensor(scratch[:, :, :], gates[:, :, :], scratch[:, :, :], ALU.subtract))
                then(dve.tensor_reduce(pair_gate[:, 0, :], scratch[:, :, :], AX.X, ALU.add))
                then(dve.tensor_copy(pair_int[:, 0, :, :], pair_slot[:, :, :]))
                then(dve.tensor_scalar(pair_int[:, 1, :, :], pair_int[:, 0, :, :], P - 1, None, ALU.bitwise_and))
                then(dve.tensor_copy(pair_place[:, :, :], pair_int[:, 1, :, :]))
                then(dve.tensor_tensor(pair_tile[:, :, :], pair_slot[:, :, :], pair_place[:, :, :], ALU.subtract))
                then(dve.tensor_scalar(pair_tile[:, :, :], pair_tile[:, :, :], 1.0 / P, None, ALU.mult))
                then(dve.tensor_tensor(ended, tile_end[:, :].unsqueeze(1).broadcast_to([P, SLOT_TILES, EXPERTS]),
                                       iota_col[:, :].unsqueeze(2).broadcast_to([P, SLOT_TILES, EXPERTS]), ALU.is_le))
                then(dve.tensor_reduce(row_tmp[:, :], ended, AX.X, ALU.add))
                then(dve.tensor_scalar(row_tmp[:, :], row_tmp[:, :], float(EXPERTS - 1), float(P), ALU.min, ALU.mult))
                then(dve.tensor_copy(tile_expert[:, 3:3 + SLOT_TILES], row_tmp[:, :]))
                dve.memset(hot_place[:, 0, :], 0.0)
                dve.memset(hot_row[:, 0, :], 0.0).then_inc(route_pe, 1)
                dve.wait_ge(route_act, 2 * layer + 2)

                slots = pair_place[:, :, :].rearrange("p w t -> p (w t)")
                tiles = pair_tile[:, :, :].rearrange("p w t -> p (w t)")

                def one_hots(i, u):
                    wait(dve, hot_used, layer * TOP * TILES + i - 3)
                    dve.tensor_scalar(hot_place[:, u, :], iota_bf[:, 0:P], slots[:, bass.ds(i, 1)], None, ALU.is_equal)
                    dve.tensor_scalar(hot_row[:, u, :], iota_bf[:, :], tiles[:, bass.ds(i, 1)], pair_row[:, bass.ds(i, 1)],
                                      ALU.is_equal, ALU.mult).then_inc(hot_ready, 1)

                staggered(dve, TOP * TILES, 4, [(0, one_hots)], back=4)
                dve.wait_ge(hot_used, (layer + 1) * TOP * TILES)
                then(dve.tensor_scalar(row_of[:, :], psum[:, 2, 0:SLOT_TILES], -1.0, None, ALU.add))
                then(dve.tensor_scalar(row_tmp[:, :], row_of[:, :], 0.0, None, ALU.is_lt))
                then(dve.tensor_tensor(row_tmp[:, :], row_tmp[:, :], spare_row[:, :], ALU.mult))
                then(dve.tensor_tensor(row_tmp[:, :], row_tmp[:, :], row_of[:, :], ALU.add))
                then(dve.tensor_copy(scatter_row[:, :], row_tmp[:, :]))
                then(dve.tensor_scalar(row_tmp[:, :], row_of[:, :], float(TILES * P), -float(TILES * P), ALU.is_ge, ALU.mult))
                then(dve.tensor_tensor(row_tmp[:, :], row_tmp[:, :], row_of[:, :], ALU.add))
                then(dve.tensor_scalar(row_tmp[:, :], row_tmp[:, :], 0.0, None, ALU.max))
                then(dve.tensor_copy(gather_row[:, :], row_tmp[:, :]))
                end_stage(dve, stage + 1)

                n0 = layer * SLOT_TILES
                registers = [dve.alloc_register(f"dve_expert_{layer}_{k}") for k in range(4)]
                norm_at = {}

                def read_experts(t):
                    dve.load(registers, tile_expert[0:1, bass.ds(t, 4)])
                    for k in range(4):
                        norm_at[k] = dve.snap(registers[k], min_val=0, max_val=(EXPERTS - 1) * P)

                def times_up(i, u):
                    dve.wait_ge(silu_done, n0 + i + 1)
                    wait(dve, act_turned, n0 + i - 1)
                    dve.tensor_tensor(act[:, u % 2, :], silu[:, u % 2, :], psum[:, 3 + u % 2, :], ALU.mult).then_inc(act_done, 1)

                def scale_slots(i, u):
                    dve.wait_ge(slot_sumsq, n0 + i + 1)
                    at = norm_at[(u + 3) % 4]
                    dve.tensor_tensor(slot_out[:, u, 0:P], psum[:, 7, 0:P], enorm[:, bass.ds(at, P)], ALU.mult).then_inc(slot_ready, 1)

                staggered(dve, SLOT_TILES, 4, [(1, times_up), (3, scale_slots)], before=read_experts)
                end_stage(dve, stage + 2)

                def mix(i, u):
                    dve.wait_ge(back_rms_ready, off + i + 1)
                    wait(dve, mix_sumsq, off + i - 1)
                    dve.reciprocal(back_scale[:, u % 2, :, :], back_rms[:, u % 2, :, :]).then_inc(back_step, 1)
                    dve.wait_ge(back_step, 3 * (off + i) + 1)
                    dve.tensor_tensor(back_scale[:, u % 2, :, :], back_scale[:, u % 2, :, :],
                                      pair_gate[:, :, bass.ds(i * QUAD, QUAD)], ALU.mult).then_inc(back_step, 1)
                    dve.wait_ge(back_step, 3 * (off + i) + 2)
                    for k in range(QUAD):
                        last = dve.tensor_scalar(scaled_lo[:, u % 2, k, :], back[:, u, 0, k, 0:P], back_scale[:, u % 2, 0, k:k + 1], None, ALU.mult)
                    last.then_inc(back_step, 1)
                    dve.wait_ge(back_step, 3 * (off + i) + 3)
                    for k in range(QUAD):
                        last = dve.scalar_tensor_tensor(out=ln[:, u % 2, k, :], in0=back[:, u, 1, k, 0:P],
                                                        scalar=back_scale[:, u % 2, 1, k:k + 1], in1=scaled_lo[:, u % 2, k, :],
                                                        op0=ALU.mult, op1=ALU.add)
                    last.then_inc(mixed, 1)

                def scale_mix(i, u):
                    dve.wait_ge(mix_rms_ready, off + i + 1)
                    dve.reciprocal(rrms[:, u % 2, :], rms[:, u % 2, :]).then_inc(mix_rrms, 1)
                    wait(dve, mix_turned, off + i - 1)
                    dve.wait_ge(mix_rrms, off + i + 1)
                    dve.tensor_tensor(h[:, u % 2, :, :], ln[:, u % 2, :, :],
                                      rrms[:, u % 2, :].unsqueeze(2).broadcast_to([P, QUAD, P]), ALU.mult).then_inc(mix_scaled, 1)

                def add_x(i, u):
                    dve.wait_ge(y_done, off + i + 1)
                    xs = x[:, bass.ds(i * QUAD, QUAD), :].rearrange("p k m -> p (k m)")
                    dve.scalar_tensor_tensor(out=xs, in0=psum[:, 2 + u % 2, :], scalar=0.5, in1=xs, op0=ALU.mult,
                                             op1=ALU.add).then_inc(x_added, 1)

                staggered(dve, GROUPS, BACK, [(6, add_x), (3, scale_mix), (1, mix)])
                end_stage(dve, stage + 3)

            def attention():
                def statistics(i, u):
                    if u % QUAD == 0:
                        q = u // QUAD
                        wait(dve, a_std, i - QUAD)
                        for k in range(QUAD):
                            last = dve.bn_stats(stats[:, q, k, :], x[:, bass.ds(i + k, 1), :].rearrange("p a m -> p (a m)"))
                        last.then_inc(a_bn, QUAD)
                        wait_apart(dve, a_bn, i + QUAD, passed)
                        for k in range(QUAD):
                            last = dve.bn_aggr(mean_var[:, q, k, :], stats[:, q, k, :])
                        last.then_inc(a_stats, QUAD)

                def normalise(i, u):
                    if u % QUAD == 0:
                        q = u // QUAD
                        dve.wait_ge(a_std, i + QUAD)
                        dve.reciprocal(rstd[:, q, :], std[:, q, :]).then_inc(a_rstd, QUAD)
                        wait(dve, a_turned, i - QUAD)
                        dve.wait_ge(a_rstd, i + QUAD)
                        for k in range(QUAD):
                            last = dve.tensor_scalar(ln[:, q, k, :], x[:, bass.ds(i + k, 1), :].rearrange("p a m -> p (a m)"),
                                                     mean_var[:, q, k, 0:1], rstd[:, q, k:k + 1], ALU.subtract, ALU.mult)
                        last.then_inc(a_normed, QUAD)

                def add_bias(i, u):
                    dve.wait_ge(qkv_done, i + 1)
                    wait(dve, a_exps, i - 1)
                    dve.tensor_tensor(qk[:, u % 2, :], psum[:, 1, 0:2 * P], bqkv[:, 0:2 * P], ALU.add)
                    wait(dve, state_done, i - 3)
                    wait(dve, kv_ready, i - 3)
                    dve.tensor_tensor(v_one[:, u % 4, :].rearrange("p (h e) -> p h e", h=HEADS)[:, :, 0:HD],
                                      psum[:, 1, 2 * P:3 * P].rearrange("p (h d) -> p h d", h=HEADS),
                                      bqkv[:, 2 * P:3 * P].rearrange("p (h d) -> p h d", h=HEADS), ALU.add).then_inc(qkv_biased, 1)

                def make_phi(i, u):
                    dve.wait_ge(a_exps, i + 1)
                    wait(dve, state_done, i - 3)
                    wait(dve, kv_ready, i - 3)
                    dve.scalar_tensor_tensor(out=phi[:, u % 4, :], in0=exps[:, u % 2, :], scalar=1.0, in1=relus[:, u % 2, :],
                                             op0=ALU.min, op1=ALU.add).then_inc(phi_ready, 1)

                def keep_state(i, u):
                    dve.wait_ge(state_done, i + 1)
                    wait(dve, inter_done, i - 2)
                    if u == CHUNK_TILES - 1:
                        dve.memset(state[:, u % 4, :], 0.0).then_inc(state_ready, 1)
                        return
                    dve.tensor_tensor(state[:, u % 4, :], psum[:, 5, 0:HEADS * HV], head_mask[:, :], ALU.mult).then_inc(state_ready, 1)

                def read_sums(i, u):
                    q = phi[:, u % 4, 0:P].rearrange("p (h d) -> p h d", h=HEADS)
                    for n, (a, b) in enumerate(THIRDS):
                        h0, h1 = a // (HV * HD), b // (HV * HD)
                        dve.wait_ge(sums_done, 3 * i + n + 1)
                        dve.tensor_tensor(read[:, u % 2, a:b].rearrange("p (h e d) -> p h e d", e=HV, d=HD),
                                          psum[:, 2 + n, 0:b - a].rearrange("p (h e d) -> p h e d", e=HV, d=HD),
                                          q[:, h0:h1, :].unsqueeze(2).broadcast_to([P, h1 - h0, HV, HD]), ALU.mult).then_inc(read_done, 1)
                    dve.wait_ge(read_done, 3 * i + 3)
                    dve.tensor_reduce(intra[:, u % 2, :], read[:, u % 2, :].rearrange("p (n d) -> p n d", d=HD), AX.X, ALU.add).then_inc(reduced, 1)

                def divide(i, u):
                    dve.wait_ge(reduced, i + 1)
                    dve.wait_ge(inter_done, i + 1)
                    dve.tensor_tensor(intra[:, u % 2, :], intra[:, u % 2, :], psum[:, 7, 0:HEADS * HV], ALU.add).then_inc(total_done, 1)
                    dve.wait_ge(total_done, i + 1)
                    both = intra[:, u % 2, :].rearrange("p (h e) -> p h e", h=HEADS)
                    dve.reciprocal(recip_den[:, u % 2, :], both[:, :, HD]).then_inc(den_done, 1)
                    dve.wait_ge(den_done, i + 1)
                    wait(dve, att_turned, i - 1)
                    dve.tensor_tensor(att[:, u % 2, :].rearrange("p (h d) -> p h d", h=HEADS), both[:, :, 0:HD],
                                      recip_den[:, u % 2, :].unsqueeze(2).broadcast_to([P, HEADS, HD]), ALU.mult).then_inc(att_ready, 1)

                def add_x(i, u):
                    dve.wait_ge(o_done, i + 1)
                    dve.wait_ge(bo_added, i + 1)
                    xt = x[:, bass.ds(i, 1), :].rearrange("p a m -> p (a m)")
                    dve.tensor_tensor(xt, psum[:, 0, 0:P], xt, ALU.add).then_inc(att_added, 1)

                staggered(dve, TILES, CHUNK_TILES, [(8, keep_state), (10, divide), (13, add_x), (5, add_bias), (9, read_sums),
                                                    (6, make_phi), (2, normalise), (0, statistics)])
                end_stage(dve, 6)

            ffn(0, 2)
            attention()
            ffn(1, 7)


def kernel(L0_attn_x, L0_attn_Wq, L0_attn_bq, L0_attn_Wk, L0_attn_bk, L0_attn_Wv, L0_attn_bv, L0_attn_Wo, L0_attn_bo,
           L0_ffn_W_in, L0_ffn_in_norm_w, L0_ffn_Wr, L0_ffn_expert_bias, L0_ffn_Wg, L0_ffn_Wu, L0_ffn_Wd,
           L0_ffn_enorm_w, L0_ffn_out_norm_w, L0_ffn_W_out):
    import concourse.bacc as bacc
    from concourse.bass_utils import run_bass_kernel_spmd

    def laid(a):
        return np.ascontiguousarray(a)

    part, col = np.arange(P)[:, None], np.arange(P)[None, :]
    tiles = np.arange(SLOT_TILES)[None, :]
    head = np.arange(HEADS * HV)[None, :] // HV
    arrays = {
        "x": laid(np.reshape(L0_attn_x, (BATCH * SEQ, P))),
        "w_in": laid(np.transpose(L0_ffn_W_in)), "w_out": laid(np.transpose(L0_ffn_W_out)),
        "wo": laid(np.transpose(L0_attn_Wo)), "wr": laid(np.transpose(L0_ffn_Wr)),
        "wqkv": laid(np.concatenate([np.transpose(L0_attn_Wq), np.transpose(L0_attn_Wk), np.transpose(L0_attn_Wv)], 1)),
        "wg": laid(np.transpose(L0_ffn_Wg, (2, 0, 1)).reshape(P, EXPERTS * FF)),
        "wu": laid(np.transpose(L0_ffn_Wu, (2, 0, 1)).reshape(P, EXPERTS * FF)),
        "wd": laid(np.transpose(np.reshape(L0_ffn_Wd, (EXPERTS, P, CHUNKS, P)), (3, 0, 2, 1)).reshape(P, EXPERTS * FF)),
        "in_norm": laid(np.reshape(L0_ffn_in_norm_w, (P, 1))), "out_norm": laid(np.reshape(L0_ffn_out_norm_w, (P, 1))),
        "enorm": laid(np.reshape(L0_ffn_enorm_w, (EXPERTS * P,))), "rbias": laid(L0_ffn_expert_bias),
        "bqkv": laid(np.concatenate([L0_attn_bq, L0_attn_bk, L0_attn_bv])), "bo": laid(L0_attn_bo),
        "ident": laid((part == col).astype(np.float32)),
        "upto_here": laid((part <= col).astype(np.float32)),
        "before_here": laid((part < col).astype(np.float32)),
        "head_mask": laid((part // HD == head).astype(np.float32)),
        "iota_col": laid(np.broadcast_to(tiles, (P, SLOT_TILES)).astype(np.float32)),
        "pair_row": laid((1 + P * np.arange(TOP * TILES)[None, :] + part).astype(np.float32)),
        "spare_row": laid((OUT_ROWS + 1 + P * tiles + part).astype(np.float32)),
    }
    nc = bacc.Bacc("TRN2", target_bir_lowering=False, num_devices=1)
    d = {n: nc.dram_tensor("in_" + n, a.shape, F32, kind="ExternalInput").ap() for n, a in arrays.items()}
    d["out"] = nc.dram_tensor("out_x", (BATCH * SEQ, P), F32, kind="ExternalOutput").ap()
    build(nc, d)
    r = run_bass_kernel_spmd(nc, [{"in_" + n: a for n, a in arrays.items()}], core_ids=[0])
    return r.results[0]["out_x"].reshape(BATCH, SEQ, P)
```

```python
from contextlib import ExitStack

import concourse.bass as bass
import concourse.mybir as mybir
import numpy as np

F32, F32R, BF16, I32 = mybir.dt.float32, mybir.dt.float32r, mybir.dt.bfloat16, mybir.dt.int32
ALU, ACT, AX = mybir.AluOpType, mybir.ActivationFunctionType, mybir.AxisListType

P = 128
BATCH, SEQ = 8, 1024
TILES = BATCH * SEQ // P
FIRST = 2
QUAD = 4
GROUPS = TILES // QUAD
EXPERTS, TOP, FF = 8, 2, 512
CHUNKS = FF // P
SLOT_TILES = TILES * TOP + EXPERTS
HEADS, HD = 16, 8
HV = HD + 1
CHUNK_TILES = SEQ // P
KV = HEADS * HV * HD
LN_EPS = 1e-5
RMS_EPS = float(np.finfo(np.float32).eps)
ROW = P + 4
BACK = 4
OUT_ROWS = TOP * TILES * P
SCATTER_LAG = 7


def wait(engine, semaphore, value):
    if not isinstance(value, int) or value > 0:
        engine.wait_ge(semaphore, value)


def wait_apart(engine, semaphore, value, passed):
    engine.wait_ge(semaphore, value)
    engine.sem_inc(passed, 1)


THIRDS = [(0, 6 * HV * HD), (6 * HV * HD, 11 * HV * HD), (11 * HV * HD, KV)]


def least(a, b):
    return a if not isinstance(a, int) else min(a, b)


def staggered(engine, count, unroll, steps, before=None, back=2):
    most = max(lag for lag, _ in steps)
    depth = -(-(most + back) // unroll) * unroll

    def turn(base, k):
        for lag, fn in steps:
            i = base + k - lag
            if not isinstance(i, int) or 0 <= i < count:
                fn(i, (k - lag) % unroll)

    for t in range(depth):
        if before and t % unroll == 0:
            before(t)
        turn(t - t % unroll, t % unroll)
    with engine.Fori(depth // unroll, count // unroll) as body:
        t = body * unroll
        if before:
            before(t)
        for k in range(unroll):
            turn(t, k)
    for t in range(count, count + most):
        if before and t % unroll == 0:
            before(t)
        turn(t - t % unroll, t % unroll)


def build(nc, d):
    with ExitStack() as ctx:
        def sb(name, shape, dt=F32):
            return ctx.enter_context(nc.sbuf_tensor(name, shape, dt))

        def sem(name):
            return ctx.enter_context(nc.semaphore(name))

        x = sb("x", [P, TILES, P])
        w_in, w_out, wo = sb("w_in", [P, P]), sb("w_out", [P, P]), sb("w_o", [P, P])
        wr = sb("w_router", [P, EXPERTS])
        wqkv = sb("w_qkv", [P, 3 * P])
        wg, wu = sb("w_gate", [P, EXPERTS * FF]), sb("w_up", [P, EXPERTS * FF])
        wd = sb("w_down", [P, EXPERTS * FF])
        in_norm, out_norm = sb("in_norm", [P, 1]), sb("out_norm", [P, 1])
        enorm = sb("enorm", [P, EXPERTS * P])
        rbias = sb("router_bias", [P, EXPERTS])
        bo = sb("b_o", [P, P])
        bias_parts, part_ones = sb("bias_parts", [P, 3 * P], F32R), sb("part_ones", [P, P], F32R)
        ident, upto_here, before_here = sb("ident", [P, P]), sb("upto_here", [P, P]), sb("before_here", [P, P])
        ones = sb("ones", [P, P])
        head_mask = sb("head_mask", [P, HEADS * HV])
        iota_col = sb("iota_col", [P, SLOT_TILES])
        iota_bf = sb("iota_bf", [P, SLOT_TILES], BF16)
        pair_row = sb("pair_row", [P, TOP * TILES])
        spare_row = sb("spare_row", [P, SLOT_TILES])
        eps_ln, eps_rms = sb("eps_ln", [P, 1]), sb("eps_rms", [P, 1])

        logits = sb("logits", [P, TILES, EXPERTS])
        gates = sb("gates", [P, TILES, EXPERTS])
        picked = sb("picked", [P, TILES, EXPERTS])
        slot_of = sb("slot_of", [P, TILES, EXPERTS])
        scratch = sb("route_scratch", [P, TILES, EXPERTS])
        wide = sb("wide", [P, BACK * TOP * QUAD * ROW])
        beats = wide[:, 0:TILES * EXPERTS * EXPERTS].rearrange("p (t a b) -> p t a b", a=EXPERTS, b=EXPERTS)
        over = wide[:, 0:EXPERTS * TILES].rearrange("p (e t) -> p e t", e=EXPERTS)
        ended = wide[:, 0:EXPERTS * SLOT_TILES].rearrange("p (t e) -> p t e", e=EXPERTS)
        read = wide[:, 0:2 * KV].rearrange("p (u n) -> p u n", u=2)
        back = wide[:, :].rearrange("p (b w k r) -> p b w k r", b=BACK, w=TOP, k=QUAD)
        per_token = sb("per_token", [P, 2, TILES])
        pair_gate = sb("pair_gate", [P, TOP, TILES])
        pair_slot = sb("pair_slot", [P, TOP, TILES])
        pair_int = sb("pair_int", [P, 2, TOP, TILES], I32)
        pair_tile, pair_place = sb("pair_tile", [P, TOP, TILES]), sb("pair_place", [P, TOP, TILES])
        picks_here = sb("picks_here", [P, EXPERTS])
        counts = sb("counts", [P, EXPERTS])
        tile_count, tile_end = sb("tile_count", [P, EXPERTS]), sb("tile_end", [P, EXPERTS])
        first_slot = sb("first_slot", [P, EXPERTS])
        hot_place, hot_row = sb("hot_place", [P, 4, P]), sb("hot_row", [P, 4, SLOT_TILES])
        row_of, row_tmp = sb("row_of", [P, SLOT_TILES]), sb("row_tmp", [P, SLOT_TILES])
        gather_row = sb("gather_row", [P, SLOT_TILES], I32)
        scatter_row = sb("scatter_row", [P, SLOT_TILES], I32)
        tile_expert = sb("tile_expert", [P, SLOT_TILES + 8], I32)

        stats = sb("stats", [P, 2, QUAD, 6])
        mean_var = sb("mean_var", [P, 2, QUAD, 2])
        std, rstd, shift = sb("std", [P, 2, QUAD]), sb("rstd", [P, 2, QUAD]), sb("shift", [P, 2, QUAD])
        ln = sb("ln", [P, 2, QUAD, P])
        ln_t = sb("ln_t", [P, 2, QUAD * P])
        squares = sb("squares", [P, 2, QUAD, P])
        scaled_lo = sb("scaled_lo", [P, 2, QUAD, P])
        sumsq, rms, rrms = sb("sumsq", [P, 2, QUAD]), sb("rms", [P, 2, QUAD]), sb("rrms", [P, 2, QUAD])
        h = sb("h", [P, 2, QUAD, P])
        h_t = sb("h_t", [P, 2, QUAD * P])
        back_rms, back_scale = sb("back_rms", [P, 2, TOP, QUAD]), sb("back_scale", [P, 2, TOP, QUAD])

        gather_now, scatter_now = sb("gather_now", [P, 4], I32), sb("scatter_now", [P, 4], I32)
        gate_now, up_now = ln[:, :, :, :].rearrange("p u k m -> p u (k m)"), ln_t
        slot_h = sb("slot_h", [P, 4, P])
        slot_ht = sb("slot_ht", [P, 2, P])
        silu = sb("silu", [P, 2, FF])
        act_t = sb("act_t", [P, 2, FF])
        slot_sq = sb("slot_sq", [P, 4, P])
        slot_out = sb("slot_out", [P, 4, ROW])

        exps, relus = sb("exps", [P, 2, 2 * P]), sb("relus", [P, 2, 2 * P])
        phi = sb("phi", [P, 4, 2 * P])
        v_one = sb("v_one", [P, 4, HEADS * HV])
        kv = sb("kv", [P, 2, KV])
        bqkv, bias_rest = kv[:, 0, 0:3 * P], kv[:, 1, 0:3 * P]
        intra = sb("intra", [P, 2, HEADS * HV])
        q_t = sb("q_t", [P, 4, P])
        state = sb("state", [P, 4, HEADS * HV])
        recip_den = sb("recip_den", [P, 2, HEADS])
        att = sb("att", [P, 2, P])
        att_t = sb("att_t", [P, 2, P])

        psum = ctx.enter_context(nc.psum_tensor("psum", [P, 8, 512], F32))
        h_dram = nc.dram_tensor("h_dram", [TILES * P, P], F32, kind="Internal").ap()
        out_dram = nc.dram_tensor("out_dram", [OUT_ROWS + SLOT_TILES * P, ROW], F32, kind="Internal").ap()

        loaded, first_loaded, rest_loaded, experts_loaded = sem("loaded"), sem("first_loaded"), sem("rest_loaded"), sem("experts_loaded")
        stage_done, passed = sem("stage_done"), sem("passed")
        x_tok = d["x"].rearrange("(t p) m -> p t m", p=P)
        out_tok = d["out"].rearrange("(t p) m -> p t m", p=P)

        bn_done, stats_done, std_ready, rstd_done = sem("bn_done"), sem("stats_done"), sem("std_ready"), sem("rstd_done")
        normed, ln_turned, ln_t_ready, h_product = sem("normed"), sem("ln_turned"), sem("ln_t_ready"), sem("h_product")
        sumsq_done, rms_ready, rrms_done, h_scaled = sem("sumsq_done"), sem("rms_ready"), sem("rrms_done"), sem("h_scaled")
        h_stored = [sem("h_stored0"), sem("h_stored1")]
        h_turned, h_t_ready, logits_done, logits_kept = sem("h_turned"), sem("h_t_ready"), sem("logits_done"), sem("logits_kept")
        route_step, route_act, route_exp, route_pe = sem("route_step"), sem("route_act"), sem("route_exp"), sem("route_pe")
        hot_ready, hot_used, rows_ready = sem("hot_ready"), sem("hot_used"), sem("rows_ready")
        gathered = [sem(f"gathered{k}") for k in range(4)]
        scattered = [sem(f"scattered{k}") for k in range(4)]
        gather_indexed, scatter_indexed = sem("gather_indexed"), sem("scatter_indexed")
        slot_turned, slot_ht_ready, gate_up = sem("slot_turned"), sem("slot_ht_ready"), sem("gate_up")
        silu_done, act_done, gate_fetched, up_fetched = sem("silu_done"), sem("act_done"), sem("gate_fetched"), sem("up_fetched")
        down_done, slot_sumsq, slot_ready = sem("down_done"), sem("slot_sumsq"), sem("slot_ready")
        back_loaded = [sem(f"back_loaded{k}") for k in range(BACK)]
        back_rms_ready, back_step, mixed = sem("back_rms_ready"), sem("back_step"), sem("mixed")
        mix_sumsq, mix_rms_ready, mix_rrms, mix_scaled = sem("mix_sumsq"), sem("mix_rms_ready"), sem("mix_rrms"), sem("mix_scaled")
        mix_turned, mix_t_ready, y_done, x_added, x_stored = sem("mix_turned"), sem("mix_t_ready"), sem("y_done"), sem("x_added"), sem("x_stored")
        a_bn, a_stats, a_std, a_rstd, a_normed = sem("a_bn"), sem("a_stats"), sem("a_std"), sem("a_rstd"), sem("a_normed")
        a_turned, a_ln_t, qkv_done, a_shift, halved = (
            sem("a_turned"), sem("a_ln_t"), sem("qkv_done"), sem("a_shift"), sem("halved"))
        a_exps, phi_ready, kv_ready, bo_added = sem("a_exps"), sem("phi_ready"), sem("kv_ready"), sem("bo_added")
        sums_done, read_done, reduced, q_turned, q_t_ready = sem("sums_done"), sem("read_done"), sem("reduced"), sem("q_turned"), sem("q_t_ready")
        state_done, state_ready, inter_done, total_done = sem("state_done"), sem("state_ready"), sem("inter_done"), sem("total_done")
        den_done, att_ready, att_turned, att_t_ready, o_done, att_added = (
            sem("den_done"), sem("att_ready"), sem("att_turned"), sem("att_t_ready"), sem("o_done"), sem("att_added"))
        ones_set, parts_made = sem("ones_set"), sem("parts_made")

        block = ctx.enter_context(nc.Block())

        def end_stage(engine, stage):
            engine.drain().then_inc(stage_done, 1)
            engine.wait_ge(stage_done, 5 * stage)

        SMALL_LOADS = [(w_in, "w_in"), (w_out, "w_out"), (wo, "wo"), (wr, "wr"), (wqkv, "wqkv"),
                       (in_norm, "in_norm"), (out_norm, "out_norm"), (ident, "ident"),
                       (upto_here, "upto_here"), (before_here, "before_here"), (head_mask, "head_mask"),
                       (iota_col, "iota_col"), (pair_row, "pair_row"),
                       (spare_row, "spare_row")]
        ROW_LOADS = [(enorm, "enorm"), (rbias, "rbias"), (bo, "bo")]
        N_LOADS = len(SMALL_LOADS) + len(ROW_LOADS) + 1

        @block.sync
        def _(sp):
            sp.dma_start(x[:, 0:QUAD * FIRST, :], x_tok[:, 0:QUAD * FIRST, :]).then_inc(first_loaded, 16)
            for dst, name in SMALL_LOADS:
                sp.dma_start(dst[:, :], d[name]).then_inc(loaded, 16)
            for dst, name in ROW_LOADS:
                sp.dma_start(dst[:, :], d[name].partition_broadcast(P)).then_inc(loaded, 16)
            sp.dma_start(bqkv, d["bqkv"].partition_broadcast(P)).then_inc(loaded, 16)
            sp.dma_start(x[:, QUAD * FIRST:TILES, :], x_tok[:, QUAD * FIRST:TILES, :]).then_inc(rest_loaded, 16)
            for dst, name in ((wg, "wg"), (wu, "wu"), (wd, "wd")):
                sp.dma_start(dst[:, :], d[name]).then_inc(experts_loaded, 16)
            end_stage(sp, 1)

            def ffn(layer, stage):
                off = layer * GROUPS

                def store_h(i, u):
                    sp.wait_ge(h_scaled, off + i + 1)
                    sp.dma_start(h_dram[bass.ds(i * (QUAD * P), QUAD * P), :].rearrange("(k p) m -> p k m", p=P),
                                 h[:, u, :, :]).then_inc(h_stored[u], 16)

                staggered(sp, GROUPS, 2, [(0, store_h)])
                for p in range(2):
                    sp.wait_ge(h_stored[p], 8 * (off + GROUPS))
                end_stage(sp, stage)
                end_stage(sp, stage + 1)
                end_stage(sp, stage + 2)

                def load_back(i, u):
                    wait(sp, mixed, off + i - 3)
                    for w in range(TOP):
                        rows = out_dram[bass.ds((i * QUAD + w * TILES) * P, QUAD * P), :]
                        sp.dma_start(back[:, u, w, :, :], rows.rearrange("(k p) m -> p k m", p=P)
                                     ).then_inc(back_loaded[u], 16)

                def store_x(i, u):
                    sp.wait_ge(x_added, off + i + 1)
                    sp.dma_start(out_tok[:, bass.ds(i * QUAD, QUAD), :], x[:, bass.ds(i * QUAD, QUAD), :]).then_inc(x_stored, 16)

                if layer == 0:
                    staggered(sp, GROUPS, BACK, [(0, load_back)], back=4)
                else:
                    staggered(sp, GROUPS, BACK, [(0, load_back), (5, store_x)], back=4)
                end_stage(sp, stage + 3)

            ffn(0, 2)
            end_stage(sp, 6)
            ffn(1, 7)
            sp.wait_ge(x_stored, 16 * GROUPS)

        @block.tensor
        def _(pe):
            end_stage(pe, 1)

            def ffn(layer, stage):
                off = layer * GROUPS

                def turn_ln(i, u):
                    pe.wait_ge(normed, off + i + 1)
                    wait(pe, ln_t_ready, off + i - 1)
                    for k in range(QUAD):
                        last = pe.transpose(psum[:, u, k * P:(k + 1) * P], ln[:, u, k, :], ident[:, :])
                    last.then_inc(ln_turned, 1)

                def product_in(i, u):
                    pe.wait_ge(ln_t_ready, off + i + 1)
                    wait(pe, h_scaled, off + i - 1)
                    for k in range(QUAD):
                        last = pe.matmul(psum[:, 2 + u, k * P:(k + 1) * P], ln_t[:, u, k * P:(k + 1) * P], w_in[:, :],
                                         start=True, stop=True)
                    last.then_inc(h_product, 1)

                def turn_h(i, u):
                    pe.wait_ge(h_scaled, off + i + 1)
                    wait(pe, h_t_ready, off + i - 1)
                    for k in range(QUAD):
                        last = pe.transpose(psum[:, 4 + u, k * P:(k + 1) * P], h[:, u, k, :], ident[:, :])
                    last.then_inc(h_turned, 1)

                def router(i, u):
                    pe.wait_ge(h_t_ready, off + i + 1)
                    wait(pe, logits_kept, off + i - 1)
                    for k in range(QUAD):
                        last = pe.matmul(psum[:, 6 + u, k * EXPERTS:(k + 1) * EXPERTS], h_t[:, u, k * P:(k + 1) * P],
                                         wr[:, :], start=True, stop=True)
                    last.then_inc(logits_done, 1)

                staggered(pe, GROUPS, 2, [(3, product_in), (2, turn_ln), (5, turn_h), (6, router)])
                end_stage(pe, stage)

                pe.wait_ge(route_pe, layer * 2 + 1)
                pe.matmul(psum[:, 0, 0:EXPERTS], before_here[:, :], picks_here[:, :], start=True, stop=True)
                pe.matmul(psum[:, 1, 0:EXPERTS], ones[:, :], picks_here[:, :], start=True, stop=True).then_inc(route_act, 1)

                def place(i, u):
                    pe.wait_ge(hot_ready, layer * TOP * TILES + i + 1)
                    pe.matmul(psum[:, 2, 0:SLOT_TILES], hot_place[:, u, :], hot_row[:, u, :],
                              start=False, stop=False, skip_group_check=True).then_inc(hot_used, 1)

                pe.wait_ge(route_pe, layer * 2 + 2)
                pe.matmul(psum[:, 2, 0:SLOT_TILES], hot_place[:, 0, :], hot_row[:, 0, :],
                          start=True, stop=False, skip_group_check=True).then_inc(route_act, 1)
                staggered(pe, TOP * TILES, 4, [(0, place)])
                end_stage(pe, stage + 1)

                pe.wait_ge(experts_loaded, 48)
                experts_off = layer * SLOT_TILES
                registers = [pe.alloc_register(f"expert_{layer}_{k}") for k in range(4)]
                weights_at = {}

                def read_experts(t):
                    pe.load(registers, tile_expert[0:1, bass.ds(t + 1, 4)])
                    for k in range(4):
                        weights_at[k] = pe.snap(registers[k], min_val=0, max_val=(EXPERTS - 1) * P)

                def turn_slots(i, u):
                    pe.wait_ge(gathered[u], 4 * (experts_off + i) - 4 * u + 16)
                    wait(pe, slot_ht_ready, experts_off + i - 1)
                    pe.transpose(psum[:, 7 * (u % 2), 0:P], slot_h[:, u, :], ident[:, :]).then_inc(slot_turned, 1)

                def gate_and_up(i, u):
                    pe.wait_ge(slot_ht_ready, experts_off + i + 1)
                    wait(pe, act_done, experts_off + i - 1)
                    pe.wait_ge(gate_fetched, experts_off + i + 1)
                    pe.wait_ge(up_fetched, experts_off + i + 1)
                    for c in range(CHUNKS):
                        pe.matmul(psum[:, 1 + u % 2, c * P:(c + 1) * P], gate_now[:, u % 2, c * P:(c + 1) * P],
                                  slot_ht[:, u % 2, :], start=True, stop=True)
                    for c in range(CHUNKS):
                        last = pe.matmul(psum[:, 3 + u % 2, c * P:(c + 1) * P], up_now[:, u % 2, c * P:(c + 1) * P],
                                         slot_ht[:, u % 2, :], start=True, stop=True)
                    last.then_inc(gate_up, 1)

                def down(i, u):
                    pe.wait_ge(act_done, experts_off + i + 1)
                    wait(pe, slot_ready, experts_off + i - 1)
                    at = weights_at[(u + 2) % 4]
                    for c in range(CHUNKS):
                        last = pe.matmul(psum[:, 5 + u % 2, 0:P], act_t[:, u % 2, c * P:(c + 1) * P], wd[:, bass.ds(at * CHUNKS + c * P, P)],
                                         start=(c == 0), stop=(c == CHUNKS - 1))
                    last.then_inc(down_done, 1)

                staggered(pe, SLOT_TILES, 4, [(0, turn_slots), (1, gate_and_up), (2, down)], before=read_experts)
                end_stage(pe, stage + 2)

                def turn_mix(i, u):
                    pe.wait_ge(mix_scaled, off + i + 1)
                    wait(pe, mix_t_ready, off + i - 1)
                    for k in range(QUAD):
                        last = pe.transpose(psum[:, u, k * P:(k + 1) * P], h[:, u, k, :], ident[:, :])
                    last.then_inc(mix_turned, 1)

                def product_out(i, u):
                    pe.wait_ge(mix_t_ready, off + i + 1)
                    wait(pe, x_added, off + i - 1)
                    for k in range(QUAD):
                        last = pe.matmul(psum[:, 2 + u, k * P:(k + 1) * P], h_t[:, u, k * P:(k + 1) * P], w_out[:, :],
                                         start=True, stop=True)
                    last.then_inc(y_done, 1)

                staggered(pe, GROUPS, 2, [(5, product_out), (4, turn_mix)])
                end_stage(pe, stage + 3)

            def attention():
                def turn_ln(i, u):
                    if u % QUAD == 0:
                        q = u // QUAD
                        pe.wait_ge(a_normed, i + QUAD)
                        wait(pe, a_ln_t, i)
                        wait(pe, att_added, i - 11)
                        for k in range(QUAD):
                            last = pe.transpose(psum[:, 0, k * P:(k + 1) * P], ln[:, q, k, :], ident[:, :])
                        last.then_inc(a_turned, QUAD)

                def product_qkv(i, u):
                    q, k = u // QUAD, u % QUAD
                    pe.wait_ge(a_ln_t, i - k + QUAD)
                    wait(pe, a_exps, i)
                    pe.matmul(psum[:, 1, 0:3 * P], ln_t[:, q, k * P:(k + 1) * P], wqkv[:, :], start=True, stop=False)
                    pe.matmul(psum[:, 1, 0:3 * P], part_ones[0:65, :], bias_parts[0:65, :], start=False, stop=True).then_inc(qkv_done, 1)

                def turn_q(i, u):
                    pe.wait_ge(phi_ready, i + 1)
                    wait(pe, q_t_ready, i)
                    wait(pe, att_t_ready, i - 4)
                    pe.transpose(psum[:, 6, 0:P], phi[:, u % 4, 0:P], ident[:, :]).then_inc(q_turned, 1)

                def add_state(i, u):
                    wait(pe, state_ready, i)
                    pe.wait_ge(phi_ready, i + 1)
                    pe.matmul(psum[:, 5, 0:HEADS * HV], phi[:, u % 4, P:2 * P], v_one[:, u % 4, :],
                              start=(u == 0), stop=(u == CHUNK_TILES - 1), skip_group_check=True).then_inc(state_done, 1)

                def sums(i, u):
                    pe.wait_ge(kv_ready, i + 1)
                    for n, (a, b) in enumerate(THIRDS):
                        wait(pe, read_done, 3 * i + n - 2)
                        pe.matmul(psum[:, 2 + n, 0:b - a], upto_here[:, :], kv[:, u % 2, a:b], start=True, stop=True).then_inc(sums_done, 1)

                def read_state(i, u):
                    pe.wait_ge(q_t_ready, i + 1)
                    wait(pe, state_ready, i)
                    wait(pe, total_done, i)
                    pe.matmul(psum[:, 7, 0:HEADS * HV], q_t[:, u % 4, :], state[:, (u + 3) % 4, :], start=True, stop=True).then_inc(inter_done, 1)

                def turn_att(i, u):
                    pe.wait_ge(att_ready, i + 1)
                    wait(pe, att_t_ready, i)
                    wait(pe, q_t_ready, least(i + 5, TILES))
                    pe.transpose(psum[:, 6, 0:P], att[:, u % 2, :], ident[:, :]).then_inc(att_turned, 1)

                def product_o(i, u):
                    pe.wait_ge(att_t_ready, i + 1)
                    wait(pe, att_added, i)
                    wait(pe, a_ln_t, least(i + 15 - (u + 3) % QUAD, TILES))
                    pe.matmul(psum[:, 0, 0:P], att_t[:, u % 2, :], wo[:, :], start=True, stop=True).then_inc(o_done, 1)

                staggered(pe, TILES, CHUNK_TILES, [(13, turn_att), (8, turn_q), (3, turn_ln), (8, sums), (4, product_qkv),
                                                   (8, add_state), (11, read_state), (14, product_o)])
                end_stage(pe, 6)

            ffn(0, 2)
            attention()
            ffn(1, 7)

        @block.scalar
        def _(act_e):
            end_stage(act_e, 1)

            def ffn(layer, stage):
                off = layer * GROUPS

                def root_variance(i, u):
                    act_e.wait_ge(stats_done, off + i + 1)
                    wait(act_e, normed, off + i - 1)
                    act_e.activation(std[:, u, :], mean_var[:, u, :, 1], ACT.Sqrt, bias=eps_ln[:, 0:1]).then_inc(std_ready, 1)

                def keep_ln_t(i, u):
                    act_e.wait_ge(ln_turned, off + i + 1)
                    wait(act_e, h_product, off + i - 1)
                    act_e.activation(ln_t[:, u, :], psum[:, u, :], ACT.Copy).then_inc(ln_t_ready, 1)

                def square_h(i, u):
                    act_e.wait_ge(h_product, off + i + 1)
                    wait(act_e, h_scaled, off + i - 1)
                    for k in range(QUAD):
                        last = act_e.activation(squares[:, u, k, :], psum[:, 2 + u, k * P:(k + 1) * P], ACT.Square,
                                                accum_out=sumsq[:, u, k:k + 1])
                    last.then_inc(sumsq_done, 1)
                    act_e.wait_ge(sumsq_done, off + i + 1)
                    act_e.activation(rms[:, u, :], sumsq[:, u, :], ACT.Sqrt, scale=1.0 / P, bias=eps_rms[:, 0:1]).then_inc(rms_ready, 1)

                def keep_h_t(i, u):
                    act_e.wait_ge(h_turned, off + i + 1)
                    wait(act_e, logits_done, off + i - 1)
                    act_e.activation(h_t[:, u, :], psum[:, 4 + u, :], ACT.Copy, scale=in_norm[:, 0:1]).then_inc(h_t_ready, 1)

                staggered(act_e, GROUPS, 2, [(3, square_h), (2, keep_ln_t), (5, keep_h_t), (0, root_variance)])
                end_stage(act_e, stage)

                act_e.wait_ge(route_exp, 2 * layer + 1)
                act_e.activation(gates[:, :, :], scratch[:, :, :], ACT.Exp).then_inc(route_exp, 1)
                end_stage(act_e, stage + 1)

                n0 = layer * SLOT_TILES

                registers = [act_e.alloc_register(f"act_expert_{layer}_{k}") for k in range(4)]
                weights_at = {}

                def read_experts(t):
                    act_e.load(registers, tile_expert[0:1, bass.ds(t + 3, 4)])
                    for k in range(4):
                        weights_at[k] = act_e.snap(registers[k], min_val=0, max_val=(EXPERTS - 1) * P)

                def fetch_up(i, u):
                    if layer == 0 and isinstance(i, int) and i == 0:
                        act_e.wait_ge(experts_loaded, 48)
                    wait(act_e, gate_up, n0 + i - 1)
                    act_e.activation(up_now[:, u % 2, :], wu[:, bass.ds(weights_at[u] * CHUNKS, FF)], ACT.Copy).then_inc(up_fetched, 1)

                def keep_slot_ht(i, u):
                    act_e.wait_ge(slot_turned, n0 + i + 1)
                    wait(act_e, gate_up, n0 + i - 1)
                    act_e.activation(slot_ht[:, u % 2, :], psum[:, 7 * (u % 2), 0:P], ACT.Copy, scale=in_norm[:, 0:1]).then_inc(slot_ht_ready, 1)

                def silu_gate(i, u):
                    act_e.wait_ge(gate_up, n0 + i + 1)
                    wait(act_e, act_done, n0 + i - 1)
                    act_e.activation(silu[:, u % 2, :], psum[:, 1 + u % 2, :], ACT.Silu).then_inc(silu_done, 1)

                def square_slots(i, u):
                    act_e.wait_ge(down_done, n0 + i + 1)
                    wait(act_e, scattered[u], 4 * (n0 + i) - 4 * u)
                    act_e.activation(slot_sq[:, u, :], psum[:, 5 + u % 2, 0:P], ACT.Square,
                                     accum_out=slot_out[:, u, P:P + 1]).then_inc(slot_sumsq, 1)

                staggered(act_e, SLOT_TILES, 4, [(0, keep_slot_ht), (0, fetch_up), (1, silu_gate), (2, square_slots)],
                          before=read_experts, back=4)
                end_stage(act_e, stage + 2)

                def root_back(i, u):
                    act_e.wait_ge(back_loaded[u], 8 * (off + i + BACK) - 8 * u)
                    wait(act_e, mixed, off + i - 1)
                    act_e.activation(back_rms[:, u % 2, :, :], back[:, u, :, :, P], ACT.Sqrt, scale=1.0 / P,
                                     bias=eps_rms[:, 0:1]).then_inc(back_rms_ready, 1)

                def square_mix(i, u):
                    act_e.wait_ge(mixed, off + i + 1)
                    wait(act_e, mix_rrms, off + i - 1)
                    for k in range(QUAD):
                        last = act_e.activation(squares[:, u % 2, k, :], ln[:, u % 2, k, :], ACT.Square,
                                                accum_out=sumsq[:, u % 2, k:k + 1])
                    last.then_inc(mix_sumsq, 1)
                    act_e.wait_ge(mix_sumsq, off + i + 1)
                    act_e.activation(rms[:, u % 2, :], sumsq[:, u % 2, :], ACT.Sqrt, scale=1.0 / P, bias=eps_rms[:, 0:1]).then_inc(mix_rms_ready, 1)

                def keep_mix_t(i, u):
                    act_e.wait_ge(mix_turned, off + i + 1)
                    wait(act_e, y_done, off + i - 1)
                    act_e.activation(h_t[:, u % 2, :], psum[:, u % 2, :], ACT.Copy, scale=out_norm[:, 0:1]).then_inc(mix_t_ready, 1)

                staggered(act_e, GROUPS, BACK, [(2, square_mix), (0, root_back), (4, keep_mix_t)])
                end_stage(act_e, stage + 3)

            def attention():
                def root_variance(i, u):
                    if u % QUAD == 0:
                        q = u // QUAD
                        act_e.wait_ge(a_stats, i + QUAD)
                        wait(act_e, a_rstd, i - QUAD)
                        act_e.activation(std[:, q, :], mean_var[:, q, :, 1], ACT.Sqrt, bias=eps_ln[:, 0:1]).then_inc(a_std, QUAD)

                def keep_ln_t(i, u):
                    if u % QUAD == 0:
                        q = u // QUAD
                        act_e.wait_ge(a_turned, i + QUAD)
                        wait(act_e, qkv_done, i - QUAD)
                        act_e.activation(ln_t[:, q, :], psum[:, 0, :], ACT.Copy).then_inc(a_ln_t, QUAD)

                def normalise(i, u):
                    if u % QUAD == 0:
                        q = u // QUAD
                        act_e.wait_ge(a_shift, i + QUAD)
                        wait(act_e, a_turned, i - QUAD)
                        for k in range(QUAD):
                            last = act_e.activation(ln[:, q, k, :], x[:, bass.ds(i + k, 1), :].rearrange("p a m -> p (a m)"),
                                                    ACT.Identity, scale=rstd[:, q, k:k + 1], bias=shift[:, q, k:k + 1])
                        last.then_inc(a_normed, QUAD)

                def elu_parts(i, u):
                    act_e.wait_ge(qkv_done, i + 1)
                    wait(act_e, phi_ready, i - 1)
                    act_e.activation(exps[:, u % 2, :], psum[:, 1, 0:2 * P], ACT.Exp)
                    act_e.activation(relus[:, u % 2, :], psum[:, 1, 0:2 * P], ACT.Relu)
                    wait(act_e, state_done, i - 3)
                    wait(act_e, kv_ready, i - 3)
                    act_e.activation(v_one[:, u % 4, :].rearrange("p (h e) -> p h e", h=HEADS)[:, :, 0:HD],
                                     psum[:, 1, 2 * P:3 * P].rearrange("p (h d) -> p h d", h=HEADS), ACT.Copy).then_inc(a_exps, 1)

                def keep_q_t(i, u):
                    act_e.wait_ge(q_turned, i + 1)
                    wait(act_e, inter_done, i - 3)
                    act_e.activation(q_t[:, u % 4, :], psum[:, 6, 0:P], ACT.Copy).then_inc(q_t_ready, 1)

                def keep_att_t(i, u):
                    act_e.wait_ge(att_turned, i + 1)
                    wait(act_e, o_done, i - 1)
                    act_e.activation(att_t[:, u % 2, :], psum[:, 6, 0:P], ACT.Copy).then_inc(att_t_ready, 1)

                staggered(act_e, TILES, CHUNK_TILES, [(13, keep_att_t), (5, elu_parts), (8, keep_q_t), (3, keep_ln_t),
                                                      (1, root_variance), (2, normalise)])
                end_stage(act_e, 6)

            ffn(0, 2)
            attention()
            ffn(1, 7)

        @block.gpsimd
        def _(pool):
            pool.memset(slot_out[:, :, :], 0.0)
            end_stage(pool, 1)

            def ffn(layer, stage):
                end_stage(pool, stage)
                end_stage(pool, stage + 1)
                n0 = layer * SLOT_TILES

                def gather(i, u):
                    wait(pool, slot_turned, n0 + i - 3)
                    pool.tensor_copy(gather_now[:, u:u + 1], gather_row[:, bass.ds(i, 1)]).then_inc(gather_indexed, 1)
                    wait_apart(pool, gather_indexed, n0 + i + 1, passed)
                    pool.indirect_dma_start(out=slot_h[:, u, :], out_offset=None, in_=h_dram[:, :],
                                            in_offset=bass.IndirectOffsetOnAxis(ap=gather_now[:, u:u + 1], axis=0)
                                            ).then_inc(gathered[u], 16)

                def scatter(i, u):
                    pool.wait_ge(slot_ready, n0 + i + 1)
                    pool.tensor_copy(scatter_now[:, u:u + 1], scatter_row[:, bass.ds(i, 1)]).then_inc(scatter_indexed, 1)
                    wait_apart(pool, scatter_indexed, n0 + i + 1, passed)
                    pool.indirect_dma_start(out=out_dram[:, :],
                                            out_offset=bass.IndirectOffsetOnAxis(ap=scatter_now[:, u:u + 1], axis=0),
                                            in_=slot_out[:, u, :], in_offset=None).then_inc(scattered[u], 16)

                staggered(pool, SLOT_TILES, 4, [(0, gather), (SCATTER_LAG, scatter)])
                for u in range(4):
                    pool.wait_ge(scattered[u], 4 * (n0 + SLOT_TILES))
                end_stage(pool, stage + 2)
                end_stage(pool, stage + 3)

            def attention():
                def products(i, u):
                    pool.wait_ge(phi_ready, i + 1)
                    wait(pool, sums_done, 3 * i - 3)
                    k = phi[:, u % 4, P:2 * P].rearrange("p (h d) -> p h d", h=HEADS)
                    v = v_one[:, u % 4, :].rearrange("p (h e) -> p h e", h=HEADS)
                    pool.tensor_tensor(kv[:, u % 2, :].rearrange("p (h e d) -> p h e d", h=HEADS, e=HV),
                                       k.unsqueeze(2).broadcast_to([P, HEADS, HV, HD]),
                                       v.unsqueeze(3).broadcast_to([P, HEADS, HV, HD]), ALU.mult).then_inc(kv_ready, 1)

                def add_bo(i, u):
                    pool.wait_ge(a_normed, i + 1)
                    xt = x[:, bass.ds(i, 1), :].rearrange("p a m -> p (a m)")
                    pool.tensor_tensor(xt, xt, bo[:, :], ALU.add).then_inc(bo_added, 1)

                def halve(i, u):
                    pool.wait_ge(read_done, 3 * i + 3)
                    pairs = read[:, u % 2, :].rearrange("p (n d) -> p n d", d=HD)
                    pool.tensor_tensor(pairs[:, :, 0:HD // 2], pairs[:, :, 0:HD // 2], pairs[:, :, HD // 2:HD], ALU.add).then_inc(halved, 1)

                staggered(pool, TILES, CHUNK_TILES, [(10, halve), (7, products), (7, add_bo)])
                end_stage(pool, 6)

            ffn(0, 2)
            attention()
            ffn(1, 7)

        @block.vector
        def _(dve):
            step = [0]
            dve.memset(ones[:, :], 1.0)
            dve.memset(v_one[:, :, :], 1.0)
            dve.memset(state[:, :, :], 0.0)
            dve.memset(tile_expert[:, :], 0)
            dve.memset(eps_ln[:, :], LN_EPS)
            dve.memset(eps_rms[:, :], RMS_EPS).then_inc(ones_set, 1)
            dve.wait_ge(loaded, 16 * N_LOADS)
            dve.tensor_copy(iota_bf[:, :], iota_col[:, :])
            made = [0]

            def parts(instruction):
                made[0] += 1
                instruction.then_inc(parts_made, 1)
                dve.wait_ge(parts_made, made[0])

            parts(dve.memset(kv[:, 0, 4 * P:5 * P], 0.0))
            for p in (0, 32, 64):
                last = dve.memset(kv[p:p + 1, 0, 4 * P:5 * P], 1.0)
            parts(last)
            parts(dve.tensor_copy(part_ones[:, :], kv[:, 0, 4 * P:5 * P]))
            parts(dve.tensor_copy(bias_parts[:, :], bqkv))
            parts(dve.tensor_tensor(bias_rest, bqkv, bias_parts[:, :], ALU.subtract))
            parts(dve.tensor_copy(bias_parts[32:64, :], kv[32:64, 1, 0:3 * P]))
            parts(dve.tensor_copy(bias_parts[64:96, :], kv[64:96, 1, 0:3 * P]))
            parts(dve.tensor_tensor(kv[64:96, 1, 0:3 * P], kv[64:96, 1, 0:3 * P], bias_parts[64:96, :], ALU.subtract))
            parts(dve.tensor_copy(bias_parts[64:96, :], kv[64:96, 1, 0:3 * P]))
            end_stage(dve, 1)

            def ffn(layer, stage):
                off = layer * GROUPS

                def statistics(i, u):
                    if layer == 0 and isinstance(i, int) and i in (0, FIRST):
                        dve.wait_ge(first_loaded if i == 0 else rest_loaded, 16)
                    wait(dve, std_ready, off + i - 1)
                    for k in range(QUAD):
                        last = dve.bn_stats(stats[:, u, k, :], x[:, bass.ds(i * QUAD + k, 1), :].rearrange("p a m -> p (a m)"))
                    last.then_inc(bn_done, 1)
                    wait_apart(dve, bn_done, off + i + 1, passed)
                    for k in range(QUAD):
                        last = dve.bn_aggr(mean_var[:, u, k, :], stats[:, u, k, :])
                    last.then_inc(stats_done, 1)

                def normalise(i, u):
                    dve.wait_ge(std_ready, off + i + 1)
                    dve.reciprocal(rstd[:, u, :], std[:, u, :]).then_inc(rstd_done, 1)
                    wait(dve, ln_turned, off + i - 1)
                    dve.wait_ge(rstd_done, off + i + 1)
                    for k in range(QUAD):
                        last = dve.tensor_scalar(ln[:, u, k, :], x[:, bass.ds(i * QUAD + k, 1), :].rearrange("p a m -> p (a m)"),
                                                 mean_var[:, u, k, 0:1], rstd[:, u, k:k + 1], ALU.subtract, ALU.mult)
                    last.then_inc(normed, 1)

                def scale_h(i, u):
                    dve.wait_ge(rms_ready, off + i + 1)
                    dve.reciprocal(rrms[:, u, :], rms[:, u, :]).then_inc(rrms_done, 1)
                    wait(dve, h_turned, off + i - 1)
                    wait(dve, h_stored[u], 8 * (off + i) - 8 * u)
                    dve.wait_ge(rrms_done, off + i + 1)
                    dve.tensor_tensor(h[:, u, :, :], psum[:, 2 + u, :].rearrange("p (k m) -> p k m", m=P),
                                      rrms[:, u, :].unsqueeze(2).broadcast_to([P, QUAD, P]), ALU.mult).then_inc(h_scaled, 1)

                def keep_logits(i, u):
                    dve.wait_ge(logits_done, off + i + 1)
                    dve.tensor_copy(logits[:, bass.ds(i * QUAD, QUAD), :].rearrange("p k e -> p (k e)"),
                                    psum[:, 6 + u, 0:QUAD * EXPERTS]).then_inc(logits_kept, 1)

                staggered(dve, GROUPS, 2, [(4, scale_h), (1, normalise), (0, statistics), (7, keep_logits)])
                end_stage(dve, stage)


                def then(instruction):
                    step[0] += 1
                    instruction.then_inc(route_step, 1)
                    dve.wait_ge(route_step, step[0])

                def over_experts(ap):
                    return ap.unsqueeze(2).broadcast_to([P, TILES, EXPERTS])

                def over_tiles(ap):
                    return ap.unsqueeze(1).broadcast_to([P, TILES, EXPERTS])

                then(dve.tensor_tensor(scratch[:, :, :], logits[:, :, :], over_tiles(rbias[:, :]), ALU.add))
                diagonal = wide[:, 0:TILES * EXPERTS * EXPERTS].rearrange("p (t n) -> p t n", t=TILES)[:, :, 0:EXPERTS * EXPERTS:EXPERTS + 1]
                then(dve.memset(diagonal, 0.0))
                for e in range(EXPERTS):
                    if e:
                        last = dve.tensor_tensor(beats[:, :, e, 0:e], scratch[:, :, 0:e],
                                                 scratch[:, :, e:e + 1].broadcast_to([P, TILES, e]), ALU.is_ge)
                    if e < EXPERTS - 1:
                        n = EXPERTS - 1 - e
                        last = dve.tensor_tensor(beats[:, :, e, e + 1:EXPERTS], scratch[:, :, e + 1:EXPERTS],
                                                 scratch[:, :, e:e + 1].broadcast_to([P, TILES, n]), ALU.is_gt)
                then(last)
                then(dve.tensor_reduce(slot_of[:, :, :], beats[:, :, :, :], AX.X, ALU.add))
                then(dve.tensor_scalar(picked[:, :, :], slot_of[:, :, :], float(TOP) - 0.5, None, ALU.is_lt))
                then(dve.tensor_scalar(scratch[:, :, :], picked[:, :, :], -1.0, 1e30, ALU.add, ALU.mult))
                then(dve.tensor_tensor(scratch[:, :, :], scratch[:, :, :], logits[:, :, :], ALU.add))
                then(dve.tensor_reduce(per_token[:, 0, :], scratch[:, :, :], AX.X, ALU.max))
                dve.tensor_tensor(scratch[:, :, :], scratch[:, :, :], over_experts(per_token[:, 0, :]),
                                  ALU.subtract).then_inc(route_exp, 1)
                dve.tensor_reduce(picks_here[:, :], picked[:, :, :].rearrange("p t e -> p e t"), AX.X, ALU.add).then_inc(route_pe, 1)
                dve.wait_ge(route_exp, 2 * layer + 2)
                then(dve.tensor_reduce(per_token[:, 0, :], gates[:, :, :], AX.X, ALU.add))
                then(dve.reciprocal(per_token[:, 1, :], per_token[:, 0, :]))
                then(dve.tensor_tensor(gates[:, :, :], gates[:, :, :], over_experts(per_token[:, 1, :]), ALU.mult))
                dve.wait_ge(route_act, 2 * layer + 1)
                then(dve.tensor_copy(counts[:, :], psum[:, 1, 0:EXPERTS]))
                then(dve.tensor_scalar(row_tmp[:, 0:TILES], iota_col[:, 0:TILES], float(P), None, ALU.mult))
                then(dve.tensor_tensor(over, counts[:, :].unsqueeze(2).broadcast_to([P, EXPERTS, TILES]),
                                       row_tmp[:, 0:TILES].unsqueeze(1).broadcast_to([P, EXPERTS, TILES]), ALU.is_gt))
                then(dve.tensor_reduce(tile_count[:, :], over, AX.X, ALU.add))
                then(dve.tensor_tensor_scan(tile_end[:, :], ones[:, 0:EXPERTS], tile_count[:, :], 0.0, ALU.mult, ALU.add))
                then(dve.tensor_tensor(first_slot[:, :], tile_end[:, :], tile_count[:, :], ALU.subtract))
                then(dve.scalar_tensor_tensor(out=first_slot[:, :], in0=first_slot[:, :], scalar=float(P),
                                              in1=psum[:, 0, 0:EXPERTS], op0=ALU.mult, op1=ALU.add))
                for e in range(EXPERTS):
                    last = dve.tensor_tensor_scan(slot_of[:, :, e], ones[:, 0:TILES], picked[:, :, e],
                                                  first_slot[:, e:e + 1], ALU.mult, ALU.add)
                then(last)
                then(dve.tensor_tensor(slot_of[:, :, :], slot_of[:, :, :], picked[:, :, :], ALU.subtract))
                then(dve.tensor_tensor(slot_of[:, :, :], slot_of[:, :, :], picked[:, :, :], ALU.mult))
                then(dve.tensor_reduce(pair_slot[:, 1, :], slot_of[:, :, :], AX.X, ALU.max))
                then(dve.tensor_reduce(per_token[:, 0, :], slot_of[:, :, :], AX.X, ALU.add))
                then(dve.tensor_tensor(pair_slot[:, 0, :], per_token[:, 0, :], pair_slot[:, 1, :], ALU.subtract))
                then(dve.tensor_tensor(scratch[:, :, :], slot_of[:, :, :], over_experts(pair_slot[:, 1, :]), ALU.is_equal))
                then(dve.tensor_tensor(scratch[:, :, :], scratch[:, :, :], gates[:, :, :], ALU.mult))
                then(dve.tensor_reduce(pair_gate[:, 1, :], scratch[:, :, :], AX.X, ALU.add))
                then(dve.tensor_tensor(scratch[:, :, :], gates[:, :, :], scratch[:, :, :], ALU.subtract))
                then(dve.tensor_reduce(pair_gate[:, 0, :], scratch[:, :, :], AX.X, ALU.add))
                then(dve.tensor_copy(pair_int[:, 0, :, :], pair_slot[:, :, :]))
                then(dve.tensor_scalar(pair_int[:, 1, :, :], pair_int[:, 0, :, :], P - 1, None, ALU.bitwise_and))
                then(dve.tensor_copy(pair_place[:, :, :], pair_int[:, 1, :, :]))
                then(dve.tensor_tensor(pair_tile[:, :, :], pair_slot[:, :, :], pair_place[:, :, :], ALU.subtract))
                then(dve.tensor_scalar(pair_tile[:, :, :], pair_tile[:, :, :], 1.0 / P, None, ALU.mult))
                then(dve.tensor_tensor(ended, tile_end[:, :].unsqueeze(1).broadcast_to([P, SLOT_TILES, EXPERTS]),
                                       iota_col[:, :].unsqueeze(2).broadcast_to([P, SLOT_TILES, EXPERTS]), ALU.is_le))
                then(dve.tensor_reduce(row_tmp[:, :], ended, AX.X, ALU.add))
                then(dve.tensor_scalar(row_tmp[:, :], row_tmp[:, :], float(EXPERTS - 1), float(P), ALU.min, ALU.mult))
                then(dve.tensor_copy(tile_expert[:, 3:3 + SLOT_TILES], row_tmp[:, :]))
                dve.memset(hot_place[:, 0, :], 0.0)
                dve.memset(hot_row[:, 0, :], 0.0).then_inc(route_pe, 1)
                dve.wait_ge(route_act, 2 * layer + 2)

                slots = pair_place[:, :, :].rearrange("p w t -> p (w t)")
                tiles = pair_tile[:, :, :].rearrange("p w t -> p (w t)")

                def one_hots(i, u):
                    wait(dve, hot_used, layer * TOP * TILES + i - 3)
                    dve.tensor_scalar(hot_place[:, u, :], iota_bf[:, 0:P], slots[:, bass.ds(i, 1)], None, ALU.is_equal)
                    dve.tensor_scalar(hot_row[:, u, :], iota_bf[:, :], tiles[:, bass.ds(i, 1)], pair_row[:, bass.ds(i, 1)],
                                      ALU.is_equal, ALU.mult).then_inc(hot_ready, 1)

                staggered(dve, TOP * TILES, 4, [(0, one_hots)], back=4)
                dve.wait_ge(hot_used, (layer + 1) * TOP * TILES)
                then(dve.tensor_scalar(row_of[:, :], psum[:, 2, 0:SLOT_TILES], -1.0, None, ALU.add))
                then(dve.tensor_scalar(row_tmp[:, :], row_of[:, :], 0.0, None, ALU.is_lt))
                then(dve.tensor_tensor(row_tmp[:, :], row_tmp[:, :], spare_row[:, :], ALU.mult))
                then(dve.tensor_tensor(row_tmp[:, :], row_tmp[:, :], row_of[:, :], ALU.add))
                then(dve.tensor_copy(scatter_row[:, :], row_tmp[:, :]))
                then(dve.tensor_scalar(row_tmp[:, :], row_of[:, :], float(TILES * P), -float(TILES * P), ALU.is_ge, ALU.mult))
                then(dve.tensor_tensor(row_tmp[:, :], row_tmp[:, :], row_of[:, :], ALU.add))
                then(dve.tensor_scalar(row_tmp[:, :], row_tmp[:, :], 0.0, None, ALU.max))
                then(dve.tensor_copy(gather_row[:, :], row_tmp[:, :]))
                end_stage(dve, stage + 1)

                n0 = layer * SLOT_TILES
                registers = [dve.alloc_register(f"dve_expert_{layer}_{k}") for k in range(6)]
                norm_at = {}

                def read_experts(t):
                    dve.load(registers, tile_expert[0:1, bass.ds(t + 1, 6)])
                    for k in range(6):
                        norm_at[k] = dve.snap(registers[k], min_val=0, max_val=(EXPERTS - 1) * P)

                def fetch_gate(i, u):
                    if layer == 0 and isinstance(i, int) and i == 0:
                        dve.wait_ge(experts_loaded, 48)
                    wait(dve, gate_up, n0 + i - 1)
                    dve.tensor_copy(gate_now[:, u % 2, :], wg[:, bass.ds(norm_at[u + 2] * CHUNKS, FF)]).then_inc(gate_fetched, 1)

                def times_up(i, u):
                    dve.wait_ge(silu_done, n0 + i + 1)
                    wait(dve, down_done, n0 + i - 1)
                    dve.tensor_tensor(act_t[:, u % 2, :], silu[:, u % 2, :], psum[:, 3 + u % 2, :], ALU.mult).then_inc(act_done, 1)

                def scale_slots(i, u):
                    dve.wait_ge(slot_sumsq, n0 + i + 1)
                    at = norm_at[(u + 2) % 4]
                    dve.tensor_tensor(slot_out[:, u, 0:P], psum[:, 5 + u % 2, 0:P], enorm[:, bass.ds(at, P)], ALU.mult).then_inc(slot_ready, 1)

                staggered(dve, SLOT_TILES, 4, [(0, fetch_gate), (1, times_up), (2, scale_slots)], before=read_experts)
                end_stage(dve, stage + 2)

                def mix(i, u):
                    dve.wait_ge(back_rms_ready, off + i + 1)
                    wait(dve, mix_sumsq, off + i - 1)
                    dve.reciprocal(back_scale[:, u % 2, :, :], back_rms[:, u % 2, :, :]).then_inc(back_step, 1)
                    dve.wait_ge(back_step, 3 * (off + i) + 1)
                    dve.tensor_tensor(back_scale[:, u % 2, :, :], back_scale[:, u % 2, :, :],
                                      pair_gate[:, :, bass.ds(i * QUAD, QUAD)], ALU.mult).then_inc(back_step, 1)
                    dve.wait_ge(back_step, 3 * (off + i) + 2)
                    for k in range(QUAD):
                        last = dve.tensor_scalar(scaled_lo[:, u % 2, k, :], back[:, u, 0, k, 0:P], back_scale[:, u % 2, 0, k:k + 1], None, ALU.mult)
                    last.then_inc(back_step, 1)
                    dve.wait_ge(back_step, 3 * (off + i) + 3)
                    for k in range(QUAD):
                        last = dve.scalar_tensor_tensor(out=ln[:, u % 2, k, :], in0=back[:, u, 1, k, 0:P],
                                                        scalar=back_scale[:, u % 2, 1, k:k + 1], in1=scaled_lo[:, u % 2, k, :],
                                                        op0=ALU.mult, op1=ALU.add)
                    last.then_inc(mixed, 1)

                def scale_mix(i, u):
                    dve.wait_ge(mix_rms_ready, off + i + 1)
                    dve.reciprocal(rrms[:, u % 2, :], rms[:, u % 2, :]).then_inc(mix_rrms, 1)
                    wait(dve, mix_turned, off + i - 1)
                    dve.wait_ge(mix_rrms, off + i + 1)
                    dve.tensor_tensor(h[:, u % 2, :, :], ln[:, u % 2, :, :],
                                      rrms[:, u % 2, :].unsqueeze(2).broadcast_to([P, QUAD, P]), ALU.mult).then_inc(mix_scaled, 1)

                def add_x(i, u):
                    dve.wait_ge(y_done, off + i + 1)
                    xs = x[:, bass.ds(i * QUAD, QUAD), :].rearrange("p k m -> p (k m)")
                    dve.scalar_tensor_tensor(out=xs, in0=psum[:, 2 + u % 2, :], scalar=0.5, in1=xs, op0=ALU.mult,
                                             op1=ALU.add).then_inc(x_added, 1)

                staggered(dve, GROUPS, BACK, [(6, add_x), (3, scale_mix), (1, mix)])
                end_stage(dve, stage + 3)

            def attention():
                def statistics(i, u):
                    if u % QUAD == 0:
                        q = u // QUAD
                        wait(dve, a_std, i - QUAD)
                        for k in range(QUAD):
                            last = dve.bn_stats(stats[:, q, k, :], x[:, bass.ds(i + k, 1), :].rearrange("p a m -> p (a m)"))
                        last.then_inc(a_bn, QUAD)
                        wait_apart(dve, a_bn, i + QUAD, passed)
                        for k in range(QUAD):
                            last = dve.bn_aggr(mean_var[:, q, k, :], stats[:, q, k, :])
                        last.then_inc(a_stats, QUAD)

                def reciprocals(i, u):
                    if u % QUAD == 0:
                        q = u // QUAD
                        dve.wait_ge(a_std, i + QUAD)
                        wait(dve, a_normed, i - QUAD)
                        dve.reciprocal(rstd[:, q, :], std[:, q, :]).then_inc(a_rstd, QUAD)
                        dve.wait_ge(a_rstd, i + QUAD)
                        dve.scalar_tensor_tensor(out=shift[:, q, :], in0=mean_var[:, q, :, 0], scalar=-1.0, in1=rstd[:, q, :],
                                                 op0=ALU.mult, op1=ALU.mult).then_inc(a_shift, QUAD)

                def make_phi(i, u):
                    dve.wait_ge(a_exps, i + 1)
                    wait(dve, state_done, i - 3)
                    wait(dve, kv_ready, i - 3)
                    dve.scalar_tensor_tensor(out=phi[:, u % 4, :], in0=exps[:, u % 2, :], scalar=1.0, in1=relus[:, u % 2, :],
                                             op0=ALU.min, op1=ALU.add).then_inc(phi_ready, 1)

                def keep_state(i, u):
                    dve.wait_ge(state_done, i + 1)
                    wait(dve, inter_done, i - 2)
                    if u == CHUNK_TILES - 1:
                        dve.memset(state[:, u % 4, :], 0.0).then_inc(state_ready, 1)
                        return
                    dve.tensor_tensor(state[:, u % 4, :], psum[:, 5, 0:HEADS * HV], head_mask[:, :], ALU.mult).then_inc(state_ready, 1)

                def read_sums(i, u):
                    q = phi[:, u % 4, 0:P].rearrange("p (h d) -> p h d", h=HEADS)
                    wait(dve, reduced, i - 1)
                    for n, (a, b) in enumerate(THIRDS):
                        h0, h1 = a // (HV * HD), b // (HV * HD)
                        dve.wait_ge(sums_done, 3 * i + n + 1)
                        dve.tensor_tensor(read[:, u % 2, a:b].rearrange("p (h e d) -> p h e d", e=HV, d=HD),
                                          psum[:, 2 + n, 0:b - a].rearrange("p (h e d) -> p h e d", e=HV, d=HD),
                                          q[:, h0:h1, :].unsqueeze(2).broadcast_to([P, h1 - h0, HV, HD]), ALU.mult).then_inc(read_done, 1)

                def reduce_sums(i, u):
                    dve.wait_ge(halved, i + 1)
                    wait(dve, att_ready, i - 1)
                    dve.tensor_reduce(intra[:, u % 2, :], read[:, u % 2, :].rearrange("p (n d) -> p n d", d=HD)[:, :, 0:HD // 2],
                                      AX.X, ALU.add).then_inc(reduced, 1)

                def add_inter(i, u):
                    dve.wait_ge(reduced, i + 1)
                    dve.wait_ge(inter_done, i + 1)
                    dve.tensor_tensor(intra[:, u % 2, :], intra[:, u % 2, :], psum[:, 7, 0:HEADS * HV], ALU.add).then_inc(total_done, 1)

                def divide(i, u):
                    dve.wait_ge(total_done, i + 1)
                    both = intra[:, u % 2, :].rearrange("p (h e) -> p h e", h=HEADS)
                    dve.reciprocal(recip_den[:, u % 2, :], both[:, :, HD]).then_inc(den_done, 1)
                    dve.wait_ge(den_done, i + 1)
                    wait(dve, att_turned, i - 1)
                    dve.tensor_tensor(att[:, u % 2, :].rearrange("p (h d) -> p h d", h=HEADS), both[:, :, 0:HD],
                                      recip_den[:, u % 2, :].unsqueeze(2).broadcast_to([P, HEADS, HD]), ALU.mult).then_inc(att_ready, 1)

                def add_x(i, u):
                    dve.wait_ge(o_done, i + 1)
                    dve.wait_ge(bo_added, i + 1)
                    xt = x[:, bass.ds(i, 1), :].rearrange("p a m -> p (a m)")
                    dve.tensor_tensor(xt, psum[:, 0, 0:P], xt, ALU.add).then_inc(att_added, 1)

                staggered(dve, TILES, CHUNK_TILES, [(11, reduce_sums), (9, read_sums), (12, add_inter), (9, keep_state), (6, make_phi), (15, add_x),
                                                    (12, divide), (2, reciprocals), (0, statistics)])
                end_stage(dve, 6)

            ffn(0, 2)
            attention()
            ffn(1, 7)


def kernel(L0_attn_x, L0_attn_Wq, L0_attn_bq, L0_attn_Wk, L0_attn_bk, L0_attn_Wv, L0_attn_bv, L0_attn_Wo, L0_attn_bo,
           L0_ffn_W_in, L0_ffn_in_norm_w, L0_ffn_Wr, L0_ffn_expert_bias, L0_ffn_Wg, L0_ffn_Wu, L0_ffn_Wd,
           L0_ffn_enorm_w, L0_ffn_out_norm_w, L0_ffn_W_out):
    import concourse.bacc as bacc
    from concourse.bass_utils import run_bass_kernel_spmd

    def laid(a):
        return np.ascontiguousarray(a)

    part, col = np.arange(P)[:, None], np.arange(P)[None, :]
    tiles = np.arange(SLOT_TILES)[None, :]
    head = np.arange(HEADS * HV)[None, :] // HV
    arrays = {
        "x": laid(np.reshape(L0_attn_x, (BATCH * SEQ, P))),
        "w_in": laid(np.transpose(L0_ffn_W_in)), "w_out": laid(np.transpose(L0_ffn_W_out)),
        "wo": laid(np.transpose(L0_attn_Wo)), "wr": laid(np.transpose(L0_ffn_Wr)),
        "wqkv": laid(np.concatenate([np.transpose(L0_attn_Wq), np.transpose(L0_attn_Wk), np.transpose(L0_attn_Wv)], 1)),
        "wg": laid(np.transpose(L0_ffn_Wg, (2, 0, 1)).reshape(P, EXPERTS * FF)),
        "wu": laid(np.transpose(L0_ffn_Wu, (2, 0, 1)).reshape(P, EXPERTS * FF)),
        "wd": laid(np.transpose(np.reshape(L0_ffn_Wd, (EXPERTS, P, CHUNKS, P)), (3, 0, 2, 1)).reshape(P, EXPERTS * FF)),
        "in_norm": laid(np.reshape(L0_ffn_in_norm_w, (P, 1))), "out_norm": laid(np.reshape(L0_ffn_out_norm_w, (P, 1))),
        "enorm": laid(np.reshape(L0_ffn_enorm_w, (EXPERTS * P,))), "rbias": laid(L0_ffn_expert_bias),
        "bqkv": laid(np.concatenate([L0_attn_bq, L0_attn_bk, L0_attn_bv])), "bo": laid(L0_attn_bo),
        "ident": laid((part == col).astype(np.float32)),
        "upto_here": laid((part <= col).astype(np.float32)),
        "before_here": laid((part < col).astype(np.float32)),
        "head_mask": laid((part // HD == head).astype(np.float32)),
        "iota_col": laid(np.broadcast_to(tiles, (P, SLOT_TILES)).astype(np.float32)),
        "pair_row": laid((1 + P * np.arange(TOP * TILES)[None, :] + part).astype(np.float32)),
        "spare_row": laid((OUT_ROWS + 1 + P * tiles + part).astype(np.float32)),
    }
    nc = bacc.Bacc("TRN2", target_bir_lowering=False, num_devices=1)
    d = {n: nc.dram_tensor("in_" + n, a.shape, F32, kind="ExternalInput").ap() for n, a in arrays.items()}
    d["out"] = nc.dram_tensor("out_x", (BATCH * SEQ, P), F32, kind="ExternalOutput").ap()
    build(nc, d)
    r = run_bass_kernel_spmd(nc, [{"in_" + n: a for n, a in arrays.items()}], core_ids=[0])
    return r.results[0]["out_x"].reshape(BATCH, SEQ, P)
```

```python
from contextlib import ExitStack

import concourse.bass as bass
import concourse.mybir as mybir
import numpy as np

F32, BF16, I32 = mybir.dt.float32, mybir.dt.bfloat16, mybir.dt.int32
ALU, ACT, AX = mybir.AluOpType, mybir.ActivationFunctionType, mybir.AxisListType

P = 128
BATCH, SEQ = 8, 1024
TILES = BATCH * SEQ // P
QUAD = 4
GROUPS = TILES // QUAD
X_PIECES = [0, 1, 2, 4, 8, GROUPS]
EXPERTS, TOP, FF = 8, 2, 512
CHUNKS = FF // P
SLOT_TILES = TILES * TOP + EXPERTS
HEADS, HD = 16, 8
HV = HD + 1
PAIR_QUADS = TOP * TILES // 4
CHUNK_TILES = SEQ // P
KV = HEADS * HV * HD
LN_EPS = 1e-5
RMS_EPS = float(np.finfo(np.float32).eps)
ROW = P + 4
BACK = 4
OUT_ROWS = TOP * TILES * P
SCATTER_LAG = 7


def wait(engine, semaphore, value):
    if not isinstance(value, int) or value > 0:
        engine.wait_ge(semaphore, value)


def wait_apart(engine, semaphore, value, passed):
    engine.wait_ge(semaphore, value)
    engine.sem_inc(passed, 1)


THIRDS = [(0, 6 * HV * HD), (6 * HV * HD, 11 * HV * HD), (11 * HV * HD, KV)]


def least(a, b):
    return a if not isinstance(a, int) else min(a, b)


def staggered(engine, count, unroll, steps, before=None, back=2):
    most = max(lag for lag, _ in steps)
    depth = -(-(most + back) // unroll) * unroll

    def turn(base, k):
        for lag, fn in steps:
            i = base + k - lag
            if not isinstance(i, int) or 0 <= i < count:
                fn(i, (k - lag) % unroll)

    for t in range(depth):
        if before and t % unroll == 0:
            before(t)
        turn(t - t % unroll, t % unroll)
    with engine.Fori(depth // unroll, count // unroll) as body:
        t = body * unroll
        if before:
            before(t)
        for k in range(unroll):
            turn(t, k)
    for t in range(count, count + most):
        if before and t % unroll == 0:
            before(t)
        turn(t - t % unroll, t % unroll)


def build(nc, d):
    with ExitStack() as ctx:
        def sb(name, shape, dt=F32):
            return ctx.enter_context(nc.sbuf_tensor(name, shape, dt))

        def sem(name):
            return ctx.enter_context(nc.semaphore(name))

        x = sb("x", [P, TILES, P])
        w_in, w_out, wo = sb("w_in", [P, P]), sb("w_out", [P, P]), sb("w_o", [P, P])
        wr = sb("w_router", [P, EXPERTS])
        wqkv = sb("w_qkv", [P, 3 * P])
        wg, wu = sb("w_gate", [P, EXPERTS * FF]), sb("w_up", [P, EXPERTS * FF])
        wd = sb("w_down", [P, EXPERTS * FF])
        in_norm, out_norm = sb("in_norm", [P, 1]), sb("out_norm", [P, 1])
        enorm = sb("enorm", [P, EXPERTS * P])
        rbias = sb("router_bias", [P, EXPERTS])
        bo = sb("b_o", [P, P])
        bias_parts, part_ones = sb("bias_parts", [P, 3 * P], BF16), sb("part_ones", [P, P], BF16)
        ident, upto_here, before_here = sb("ident", [P, P]), sb("upto_here", [P, P]), sb("before_here", [P, P])
        ones = sb("ones", [P, P])
        head_mask = sb("head_mask", [P, HEADS * HV])
        iota_col = sb("iota_col", [P, SLOT_TILES])
        iota_bf = sb("iota_bf", [P, SLOT_TILES], BF16)
        pair_row = sb("pair_row", [P, TOP * TILES])
        spare_row = sb("spare_row", [P, SLOT_TILES])
        eps_ln, eps_rms, table_trial = sb("eps_ln", [P, 1]), sb("eps_rms", [P, 1]), sb("table_trial", [P, 1])

        logits = sb("logits", [P, TILES, EXPERTS])
        gates = sb("gates", [P, TILES, EXPERTS])
        picked = sb("picked", [P, TILES, EXPERTS])
        slot_of = sb("slot_of", [P, TILES, EXPERTS])
        scratch = sb("route_scratch", [P, TILES, EXPERTS])
        wide = sb("wide", [P, BACK * TOP * QUAD * ROW])
        beats = wide[:, 0:TILES * EXPERTS * EXPERTS // 2].bitcast(BF16).rearrange("p (t a b) -> p t a b", a=EXPERTS, b=EXPERTS)
        over = wide[:, 0:EXPERTS * TILES].rearrange("p (e t) -> p e t", e=EXPERTS)
        ended = wide[:, 0:EXPERTS * SLOT_TILES].rearrange("p (t e) -> p t e", e=EXPERTS)
        read = wide[:, 0:2 * KV].rearrange("p (u n) -> p u n", u=2)
        back = wide[:, :].rearrange("p (b w k r) -> p b w k r", b=BACK, w=TOP, k=QUAD)
        per_token = sb("per_token", [P, 2, TILES])
        pair_gate = sb("pair_gate", [P, TOP, TILES])
        pair_slot = sb("pair_slot", [P, TOP, TILES])
        pair_int = sb("pair_int", [P, 2, TOP, TILES], I32)
        pair_tile, pair_place = sb("pair_tile", [P, TOP, TILES]), sb("pair_place", [P, TOP, TILES])
        picks_here = sb("picks_here", [P, EXPERTS])
        counts = sb("counts", [P, EXPERTS])
        tile_count, tile_end = sb("tile_count", [P, EXPERTS]), sb("tile_end", [P, EXPERTS])
        first_slot = sb("first_slot", [P, EXPERTS])
        hot_place, hot_row = sb("hot_place", [P, 8, P]), sb("hot_row", [P, 8, SLOT_TILES])
        hot_tile, tile_distance = sb("hot_tile", [P, 2, 3, SLOT_TILES], BF16), sb("tile_distance", [P, 2, SLOT_TILES], BF16)
        less_row = sb("less_row", [P, TOP * TILES])
        row_of, row_tmp = sb("row_of", [P, SLOT_TILES]), sb("row_tmp", [P, SLOT_TILES])
        gather_row = sb("gather_row", [P, SLOT_TILES], I32)
        scatter_row = sb("scatter_row", [P, SLOT_TILES], I32)
        tile_expert = sb("tile_expert", [P, SLOT_TILES + 8], I32)

        stats = sb("stats", [P, 2, QUAD, 6])
        mean_var = sb("mean_var", [P, 2, QUAD, 2])
        std, rstd, shift = sb("std", [P, 2, QUAD]), sb("rstd", [P, 2, QUAD]), sb("shift", [P, 2, QUAD])
        ln = sb("ln", [P, 2, QUAD, P])
        ln_t = sb("ln_t", [P, 2, QUAD * P])
        squares = sb("squares", [P, 2, QUAD, P])
        scaled_first = sb("scaled_first", [P, 2, QUAD, P])
        sumsq, rms, rrms = sb("sumsq", [P, 2, QUAD]), sb("rms", [P, 2, QUAD]), sb("rrms", [P, 2, QUAD])
        h = sb("h", [P, 2, QUAD, P])
        h_t = sb("h_t", [P, 2, QUAD * P])
        back_rms, back_scale = sb("back_rms", [P, 2, TOP, QUAD]), sb("back_scale", [P, 2, TOP, QUAD])

        gather_now, scatter_now = sb("gather_now", [P, 4], I32), sb("scatter_now", [P, 4], I32)
        gate_now, up_now = ln[:, :, :, :].rearrange("p u k m -> p u (k m)"), ln_t
        slot_h = sb("slot_h", [P, 4, P])
        slot_ht = sb("slot_ht", [P, 2, P])
        silu = sb("silu", [P, 2, FF])
        act_t = sb("act_t", [P, 2, FF])
        slot_sq = sb("slot_sq", [P, 4, P])
        slot_out = sb("slot_out", [P, 4, ROW])

        exps, relus = sb("exps", [P, 2, 2 * P]), sb("relus", [P, 2, 2 * P])
        phi = sb("phi", [P, 4, 2 * P])
        v_one = sb("v_one", [P, 4, HEADS * HV])
        kv = sb("kv", [P, 2, KV])
        bqkv, bias_rest = kv[:, 0, 0:3 * P], kv[:, 1, 0:3 * P]
        intra = sb("intra", [P, 2, HEADS * HV])
        q_t = sb("q_t", [P, 4, P])
        state = sb("state", [P, 4, HEADS * HV])
        recip_den = sb("recip_den", [P, 2, HEADS])
        att = sb("att", [P, 2, P])
        att_t = sb("att_t", [P, 2, P])

        psum = ctx.enter_context(nc.psum_tensor("psum", [P, 8, 512], F32))
        h_dram = nc.dram_tensor("h_dram", [TILES * P, P], F32, kind="Internal").ap()
        out_dram = nc.dram_tensor("out_dram", [OUT_ROWS + SLOT_TILES * P, ROW], F32, kind="Internal").ap()

        early_loaded, loaded, experts_loaded = sem("early_loaded"), sem("loaded"), sem("experts_loaded")
        x_loaded = [sem(f"x_loaded{n}") for n in range(len(X_PIECES) - 1)]
        stage_done, passed = sem("stage_done"), sem("passed")
        x_tok = d["x"].rearrange("(t p) m -> p t m", p=P)
        out_tok = d["out"].rearrange("(t p) m -> p t m", p=P)

        bn_done, stats_done, std_ready, rstd_done = sem("bn_done"), sem("stats_done"), sem("std_ready"), sem("rstd_done")
        normed, ln_turned, ln_t_ready, h_product = sem("normed"), sem("ln_turned"), sem("ln_t_ready"), sem("h_product")
        sumsq_done, rms_ready, rrms_done, h_scaled = sem("sumsq_done"), sem("rms_ready"), sem("rrms_done"), sem("h_scaled")
        h_stored = [sem("h_stored0"), sem("h_stored1")]
        h_turned, h_t_ready, logits_done, logits_kept = sem("h_turned"), sem("h_t_ready"), sem("logits_done"), sem("logits_kept")
        route_step, route_act, route_exp, route_pe = sem("route_step"), sem("route_act"), sem("route_exp"), sem("route_pe")
        hot_ready, hot_used, hot_marked, distance_ready = sem("hot_ready"), sem("hot_used"), sem("hot_marked"), sem("distance_ready")
        act_rows, pool_rows, centred, first_scaled = sem("act_rows"), sem("pool_rows"), sem("centred"), sem("first_scaled")
        gathered = [sem(f"gathered{k}") for k in range(4)]
        scattered = [sem(f"scattered{k}") for k in range(4)]
        gather_indexed, scatter_indexed = sem("gather_indexed"), sem("scatter_indexed")
        slot_turned, slot_ht_ready, gate_up = sem("slot_turned"), sem("slot_ht_ready"), sem("gate_up")
        silu_done, act_done, gate_fetched, up_fetched = sem("silu_done"), sem("act_done"), sem("gate_fetched"), sem("up_fetched")
        down_done, slot_sumsq, slot_ready = sem("down_done"), sem("slot_sumsq"), sem("slot_ready")
        back_loaded = [sem(f"back_loaded{k}") for k in range(BACK)]
        back_rms_ready, back_step, mixed = sem("back_rms_ready"), sem("back_step"), sem("mixed")
        mix_sumsq, mix_rms_ready, mix_rrms, mix_scaled = sem("mix_sumsq"), sem("mix_rms_ready"), sem("mix_rrms"), sem("mix_scaled")
        mix_turned, mix_t_ready, y_done, x_added, x_stored = sem("mix_turned"), sem("mix_t_ready"), sem("y_done"), sem("x_added"), sem("x_stored")
        a_bn, a_stats, a_std, a_rstd, a_normed = sem("a_bn"), sem("a_stats"), sem("a_std"), sem("a_rstd"), sem("a_normed")
        a_turned, a_ln_t, qkv_done, a_shift, halved = (
            sem("a_turned"), sem("a_ln_t"), sem("qkv_done"), sem("a_shift"), sem("halved"))
        a_exps, phi_ready, kv_ready, bo_added = sem("a_exps"), sem("phi_ready"), sem("kv_ready"), sem("bo_added")
        sums_done, read_done, reduced, q_turned, q_t_ready = sem("sums_done"), sem("read_done"), sem("reduced"), sem("q_turned"), sem("q_t_ready")
        state_done, state_ready, inter_done, total_done = sem("state_done"), sem("state_ready"), sem("inter_done"), sem("total_done")
        den_done, att_ready, att_turned, att_t_ready, o_done, att_added = (
            sem("den_done"), sem("att_ready"), sem("att_turned"), sem("att_t_ready"), sem("o_done"), sem("att_added"))
        ones_set, parts_made = sem("ones_set"), sem("parts_made")

        block = ctx.enter_context(nc.Block())

        def end_stage(engine, stage):
            engine.drain().then_inc(stage_done, 1)
            engine.wait_ge(stage_done, 5 * stage)

        EARLY_LOADS = [(ident, "ident"), (w_in, "w_in"), (in_norm, "in_norm"), (wr, "wr")]
        LATER_LOADS = [(w_out, "w_out"), (wo, "wo"), (wqkv, "wqkv"), (out_norm, "out_norm"),
                       (upto_here, "upto_here"), (before_here, "before_here"), (head_mask, "head_mask"),
                       (iota_col, "iota_col"), (pair_row, "pair_row"), (spare_row, "spare_row")]
        ROW_LOADS = [(enorm[:, :], "enorm"), (rbias[:, :], "rbias"), (bqkv, "bqkv"), (bo[:, :], "bo")]
        N_LATER = len(LATER_LOADS) + len(ROW_LOADS)

        @block.sync
        def _(sp):
            def load_x(n):
                a, b = QUAD * X_PIECES[n], QUAD * X_PIECES[n + 1]
                sp.dma_start(x[:, a:b, :], x_tok[:, a:b, :]).then_inc(x_loaded[n], 16)

            load_x(0)
            for dst, name in EARLY_LOADS:
                sp.dma_start(dst[:, :], d[name]).then_inc(early_loaded, 16)
            end_stage(sp, 1)
            for n in range(1, len(X_PIECES) - 1):
                load_x(n)
            for dst, name in LATER_LOADS:
                sp.dma_start(dst[:, :], d[name]).then_inc(loaded, 16)
            for dst, name in ROW_LOADS:
                sp.dma_start(dst, d[name].partition_broadcast(P)).then_inc(loaded, 16)

            def ffn(layer, stage):
                off = layer * GROUPS

                def store_h(i, u):
                    sp.wait_ge(h_scaled, off + i + 1)
                    sp.dma_start(h_dram[bass.ds(i * (QUAD * P), QUAD * P), :].rearrange("(k p) m -> p k m", p=P),
                                 h[:, u, :, :]).then_inc(h_stored[u], 16)

                staggered(sp, GROUPS, 2, [(0, store_h)])
                if layer == 0:
                    for dst, name in ((wg, "wg"), (wu, "wu"), (wd, "wd")):
                        sp.dma_start(dst[:, :], d[name]).then_inc(experts_loaded, 16)
                for p in range(2):
                    sp.wait_ge(h_stored[p], 8 * (off + GROUPS))
                end_stage(sp, stage)
                end_stage(sp, stage + 1)
                end_stage(sp, stage + 2)

                def load_back(i, u):
                    wait(sp, mixed, off + i - 3)
                    for w in range(TOP):
                        rows = out_dram[bass.ds((i * QUAD + w * TILES) * P, QUAD * P), :]
                        sp.dma_start(back[:, u, w, :, :], rows.rearrange("(k p) m -> p k m", p=P)
                                     ).then_inc(back_loaded[u], 16)

                def store_x(i, u):
                    sp.wait_ge(x_added, off + i + 1)
                    sp.dma_start(out_tok[:, bass.ds(i * QUAD, QUAD), :], x[:, bass.ds(i * QUAD, QUAD), :]).then_inc(x_stored, 16)

                if layer == 0:
                    staggered(sp, GROUPS, BACK, [(0, load_back)], back=4)
                else:
                    staggered(sp, GROUPS, BACK, [(0, load_back), (10, store_x)])
                end_stage(sp, stage + 3)

            ffn(0, 2)
            end_stage(sp, 6)
            ffn(1, 7)
            sp.wait_ge(x_stored, 16 * GROUPS)

        @block.tensor
        def _(pe):
            end_stage(pe, 1)

            def ffn(layer, stage):
                off = layer * GROUPS

                def turn_ln(i, u):
                    pe.wait_ge(normed, off + i + 1)
                    wait(pe, ln_t_ready, off + i - 1)
                    for k in range(QUAD):
                        last = pe.transpose(psum[:, u, k * P:(k + 1) * P], ln[:, u, k, :], ident[:, :])
                    last.then_inc(ln_turned, 1)

                def product_in(i, u):
                    pe.wait_ge(ln_t_ready, off + i + 1)
                    wait(pe, h_scaled, off + i - 1)
                    for k in range(QUAD):
                        last = pe.matmul(psum[:, 2 + u, k * P:(k + 1) * P], ln_t[:, u, k * P:(k + 1) * P], w_in[:, :],
                                         start=True, stop=True)
                    last.then_inc(h_product, 1)

                def turn_h(i, u):
                    pe.wait_ge(h_scaled, off + i + 1)
                    wait(pe, h_t_ready, off + i - 1)
                    for k in range(QUAD):
                        last = pe.transpose(psum[:, 4 + u, k * P:(k + 1) * P], h[:, u, k, :], ident[:, :])
                    last.then_inc(h_turned, 1)

                def router(i, u):
                    pe.wait_ge(h_t_ready, off + i + 1)
                    wait(pe, logits_kept, off + i - 1)
                    for k in range(QUAD):
                        last = pe.matmul(psum[:, 6 + u, k * EXPERTS:(k + 1) * EXPERTS], h_t[:, u, k * P:(k + 1) * P],
                                         wr[:, :], start=True, stop=True)
                    last.then_inc(logits_done, 1)

                staggered(pe, GROUPS, 2, [(3, turn_ln), (6, turn_h), (4, product_in), (7, router)])
                end_stage(pe, stage)

                pe.wait_ge(route_pe, layer * 2 + 1)
                pe.matmul(psum[:, 0, 0:EXPERTS], before_here[:, :], picks_here[:, :], start=True, stop=True)
                pe.matmul(psum[:, 1, 0:EXPERTS], ones[:, :], picks_here[:, :], start=True, stop=True).then_inc(route_act, 1)

                def place(j, u):
                    done = layer * PAIR_QUADS + j + 1
                    pe.wait_ge(hot_ready, done)
                    pe.wait_ge(pool_rows, done)
                    for k in range(4):
                        if k == 3:
                            pe.wait_ge(act_rows, done)
                        last = pe.matmul(psum[:, 2, 0:SLOT_TILES], hot_place[:, 4 * u + k, :], hot_row[:, 4 * u + k, :],
                                         start=False, stop=False, skip_group_check=True)
                    last.then_inc(hot_used, 1)

                pe.wait_ge(route_pe, layer * 2 + 2)
                pe.matmul(psum[:, 2, 0:SLOT_TILES], hot_place[:, 0, :], hot_row[:, 0, :],
                          start=True, stop=False, skip_group_check=True).then_inc(route_act, 1)
                staggered(pe, PAIR_QUADS, 2, [(0, place)])
                end_stage(pe, stage + 1)

                pe.wait_ge(experts_loaded, 48)
                experts_off = layer * SLOT_TILES
                registers = [pe.alloc_register(f"expert_{layer}_{k}") for k in range(4)]
                weights_at = {}

                def read_experts(t):
                    pe.load(registers, tile_expert[0:1, bass.ds(t + 1, 4)])
                    for k in range(4):
                        weights_at[k] = pe.snap(registers[k], min_val=0, max_val=(EXPERTS - 1) * P)

                def turn_slots(i, u):
                    pe.wait_ge(gathered[u], 4 * (experts_off + i) - 4 * u + 16)
                    wait(pe, slot_ht_ready, experts_off + i - 1)
                    pe.transpose(psum[:, 7 * (u % 2), 0:P], slot_h[:, u, :], ident[:, :]).then_inc(slot_turned, 1)

                def gate_and_up(i, u):
                    pe.wait_ge(slot_ht_ready, experts_off + i + 1)
                    wait(pe, act_done, experts_off + i - 1)
                    pe.wait_ge(gate_fetched, experts_off + i + 1)
                    pe.wait_ge(up_fetched, experts_off + i + 1)
                    for c in range(CHUNKS):
                        pe.matmul(psum[:, 1 + u % 2, c * P:(c + 1) * P], gate_now[:, u % 2, c * P:(c + 1) * P],
                                  slot_ht[:, u % 2, :], start=True, stop=True)
                    for c in range(CHUNKS):
                        last = pe.matmul(psum[:, 3 + u % 2, c * P:(c + 1) * P], up_now[:, u % 2, c * P:(c + 1) * P],
                                         slot_ht[:, u % 2, :], start=True, stop=True)
                    last.then_inc(gate_up, 1)

                def down(i, u):
                    pe.wait_ge(act_done, experts_off + i + 1)
                    wait(pe, slot_ready, experts_off + i - 1)
                    at = weights_at[(u + 2) % 4]
                    for c in range(CHUNKS):
                        last = pe.matmul(psum[:, 5 + u % 2, 0:P], act_t[:, u % 2, c * P:(c + 1) * P], wd[:, bass.ds(at * CHUNKS + c * P, P)],
                                         start=(c == 0), stop=(c == CHUNKS - 1))
                    last.then_inc(down_done, 1)

                staggered(pe, SLOT_TILES, 4, [(0, turn_slots), (1, gate_and_up), (2, down)], before=read_experts)
                end_stage(pe, stage + 2)

                def turn_mix(i, u):
                    pe.wait_ge(mix_scaled, off + i + 1)
                    wait(pe, mix_t_ready, off + i - 1)
                    for k in range(QUAD):
                        last = pe.transpose(psum[:, u, k * P:(k + 1) * P], h[:, u, k, :], ident[:, :])
                    last.then_inc(mix_turned, 1)

                def product_out(i, u):
                    pe.wait_ge(mix_t_ready, off + i + 1)
                    wait(pe, x_added, off + i - 1)
                    for k in range(QUAD):
                        last = pe.matmul(psum[:, 2 + u, k * P:(k + 1) * P], h_t[:, u, k * P:(k + 1) * P], w_out[:, :],
                                         start=True, stop=True)
                    last.then_inc(y_done, 1)

                staggered(pe, GROUPS, 2, [(5, turn_mix), (6, product_out)])
                end_stage(pe, stage + 3)

            def attention():
                def turn_ln(i, u):
                    pe.wait_ge(a_normed, i + 1)
                    wait(pe, a_ln_t, i)
                    wait(pe, att_added, i - 11)
                    pe.transpose(psum[:, 0, 0:P], ln[:, u // QUAD, u % QUAD, :], ident[:, :]).then_inc(a_turned, 1)

                def product_qkv(i, u):
                    q, k = u // QUAD, u % QUAD
                    pe.wait_ge(a_ln_t, i + 1)
                    wait(pe, a_exps, i)
                    pe.matmul(psum[:, 1, 0:3 * P], ln_t[:, q, k * P:(k + 1) * P], wqkv[:, :], start=True, stop=False)
                    pe.matmul(psum[:, 1, 0:3 * P], part_ones[0:65, :], bias_parts[0:65, :], start=False, stop=True).then_inc(qkv_done, 1)

                def turn_q(i, u):
                    pe.wait_ge(phi_ready, i + 1)
                    wait(pe, q_t_ready, i)
                    wait(pe, att_t_ready, i - 5)
                    pe.transpose(psum[:, 6, 0:P], phi[:, u % 4, 0:P], ident[:, :]).then_inc(q_turned, 1)

                def add_state(i, u):
                    wait(pe, state_ready, i)
                    pe.wait_ge(phi_ready, i + 1)
                    pe.matmul(psum[:, 5, 0:HEADS * HV], phi[:, u % 4, P:2 * P], v_one[:, u % 4, :],
                              start=(u == 0), stop=(u == CHUNK_TILES - 1), skip_group_check=True).then_inc(state_done, 1)

                def sums(i, u):
                    pe.wait_ge(kv_ready, i + 1)
                    for n, (a, b) in enumerate(THIRDS):
                        wait(pe, read_done, 3 * i + n - 2)
                        pe.matmul(psum[:, 2 + n, 0:b - a], upto_here[:, :], kv[:, u % 2, a:b], start=True, stop=True).then_inc(sums_done, 1)

                def read_state(i, u):
                    pe.wait_ge(q_t_ready, i + 1)
                    wait(pe, state_ready, i)
                    wait(pe, total_done, i)
                    pe.matmul(psum[:, 7, 0:HEADS * HV], q_t[:, u % 4, :], state[:, (u + 3) % 4, :], start=True, stop=True).then_inc(inter_done, 1)

                def turn_att(i, u):
                    pe.wait_ge(att_ready, i + 1)
                    wait(pe, att_t_ready, i)
                    wait(pe, q_t_ready, least(i + 6, TILES))
                    pe.transpose(psum[:, 6, 0:P], att[:, u % 2, :], ident[:, :]).then_inc(att_turned, 1)

                def product_o(i, u):
                    pe.wait_ge(att_t_ready, i + 1)
                    wait(pe, att_added, i)
                    wait(pe, a_ln_t, least(i + 12, TILES))
                    pe.matmul(psum[:, 0, 0:P], att_t[:, u % 2, :], wo[:, :], start=True, stop=True).then_inc(o_done, 1)

                staggered(pe, TILES, CHUNK_TILES, [(15, turn_q), (15, sums), (20, turn_att), (10, turn_ln), (11, product_qkv),
                                                   (15, add_state), (18, read_state), (21, product_o)])
                end_stage(pe, 6)

            ffn(0, 2)
            attention()
            ffn(1, 7)

        @block.scalar
        def _(act_e):
            def load_table(function):
                act_e.activation(table_trial[:, :], eps_rms[:, :], function)

            act_e.wait_ge(ones_set, 1)
            end_stage(act_e, 1)

            def ffn(layer, stage):
                off = layer * GROUPS

                def root_variance(i, u):
                    act_e.wait_ge(stats_done, off + i + 1)
                    wait(act_e, normed, off + i - 1)
                    act_e.activation(std[:, u, :], mean_var[:, u, :, 1], ACT.Sqrt, bias=eps_ln[:, 0:1]).then_inc(std_ready, 1)

                def keep_ln_t(i, u):
                    act_e.wait_ge(ln_turned, off + i + 1)
                    wait(act_e, h_product, off + i - 1)
                    act_e.activation(ln_t[:, u, :], psum[:, u, :], ACT.Copy).then_inc(ln_t_ready, 1)

                def square_h(i, u):
                    act_e.wait_ge(h_product, off + i + 1)
                    wait(act_e, h_scaled, off + i - 1)
                    for k in range(QUAD):
                        last = act_e.activation(squares[:, u, k, :], psum[:, 2 + u, k * P:(k + 1) * P], ACT.Square,
                                                accum_out=sumsq[:, u, k:k + 1])
                    last.then_inc(sumsq_done, 1)
                    act_e.wait_ge(sumsq_done, off + i + 1)
                    act_e.activation(rms[:, u, :], sumsq[:, u, :], ACT.Sqrt, scale=1.0 / P, bias=eps_rms[:, 0:1]).then_inc(rms_ready, 1)

                def keep_h_t(i, u):
                    act_e.wait_ge(h_turned, off + i + 1)
                    wait(act_e, logits_done, off + i - 1)
                    act_e.activation(h_t[:, u, :], psum[:, 4 + u, :], ACT.Copy, scale=in_norm[:, 0:1]).then_inc(h_t_ready, 1)

                load_table(ACT.Sqrt)
                staggered(act_e, GROUPS, 2, [(3, keep_ln_t), (6, keep_h_t), (4, square_h), (0, root_variance)])
                end_stage(act_e, stage)


                tiles = pair_tile[:, :, :].rearrange("p w t -> p (w t)")

                def hot_rows(j, u):
                    wait(act_e, hot_used, layer * PAIR_QUADS + j - 1)
                    act_e.activation(tile_distance[:, u, :], iota_bf[:, :], ACT.Abs, scale=-1.0,
                                     bias=tiles[:, bass.ds(j * 4 + 3, 1)]).then_inc(distance_ready, 1)
                    act_e.wait_ge(distance_ready, layer * PAIR_QUADS + j + 1)
                    act_e.activation(hot_row[:, 4 * u + 3, :], tile_distance[:, u, :], ACT.Relu, scale=less_row[:, bass.ds(j * 4 + 3, 1)],
                                     bias=pair_row[:, bass.ds(j * 4 + 3, 1)]).then_inc(act_rows, 1)

                act_e.wait_ge(route_pe, 2 * layer + 2)
                staggered(act_e, PAIR_QUADS, 2, [(0, hot_rows)])
                end_stage(act_e, stage + 1)

                n0 = layer * SLOT_TILES

                registers = [act_e.alloc_register(f"act_expert_{layer}_{k}") for k in range(4)]
                weights_at = {}

                def read_experts(t):
                    act_e.load(registers, tile_expert[0:1, bass.ds(t + 3, 4)])
                    for k in range(4):
                        weights_at[k] = act_e.snap(registers[k], min_val=0, max_val=(EXPERTS - 1) * P)

                def fetch_up(i, u):
                    if layer == 0 and isinstance(i, int) and i == 0:
                        act_e.wait_ge(experts_loaded, 48)
                    wait(act_e, gate_up, n0 + i - 1)
                    act_e.activation(up_now[:, u % 2, :], wu[:, bass.ds(weights_at[u] * CHUNKS, FF)], ACT.Copy).then_inc(up_fetched, 1)

                def keep_slot_ht(i, u):
                    act_e.wait_ge(slot_turned, n0 + i + 1)
                    wait(act_e, gate_up, n0 + i - 1)
                    act_e.activation(slot_ht[:, u % 2, :], psum[:, 7 * (u % 2), 0:P], ACT.Copy, scale=in_norm[:, 0:1]).then_inc(slot_ht_ready, 1)

                def silu_gate(i, u):
                    act_e.wait_ge(gate_up, n0 + i + 1)
                    wait(act_e, act_done, n0 + i - 1)
                    act_e.activation(silu[:, u % 2, :], psum[:, 1 + u % 2, :], ACT.Silu).then_inc(silu_done, 1)

                def square_slots(i, u):
                    act_e.wait_ge(down_done, n0 + i + 1)
                    wait(act_e, scattered[u], 4 * (n0 + i) - 4 * u)
                    act_e.activation(slot_sq[:, u, :], psum[:, 5 + u % 2, 0:P], ACT.Square,
                                     accum_out=slot_out[:, u, P:P + 1]).then_inc(slot_sumsq, 1)

                load_table(ACT.Silu)
                staggered(act_e, SLOT_TILES, 4, [(0, keep_slot_ht), (0, fetch_up), (1, silu_gate), (2, square_slots)],
                          before=read_experts, back=4)

                load_table(ACT.Exp)
                act_e.wait_ge(route_exp, 2 * layer + 1)
                act_e.activation(gates[:, :, :], scratch[:, :, :], ACT.Exp).then_inc(route_exp, 1)
                end_stage(act_e, stage + 2)

                def root_back(i, u):
                    act_e.wait_ge(back_loaded[u], 8 * (off + i + BACK) - 8 * u)
                    wait(act_e, mixed, off + i - 1)
                    act_e.activation(back_rms[:, u % 2, :, :], back[:, u, :, :, P], ACT.Sqrt, scale=1.0 / P,
                                     bias=eps_rms[:, 0:1]).then_inc(back_rms_ready, 1)

                def square_mix(i, u):
                    act_e.wait_ge(mixed, off + i + 1)
                    wait(act_e, mix_rrms, off + i - 1)
                    for k in range(QUAD):
                        last = act_e.activation(squares[:, u % 2, k, :], ln[:, u % 2, k, :], ACT.Square,
                                                accum_out=sumsq[:, u % 2, k:k + 1])
                    last.then_inc(mix_sumsq, 1)
                    act_e.wait_ge(mix_sumsq, off + i + 1)
                    act_e.activation(rms[:, u % 2, :], sumsq[:, u % 2, :], ACT.Sqrt, scale=1.0 / P, bias=eps_rms[:, 0:1]).then_inc(mix_rms_ready, 1)

                def keep_mix_t(i, u):
                    act_e.wait_ge(mix_turned, off + i + 1)
                    wait(act_e, y_done, off + i - 1)
                    act_e.activation(h_t[:, u % 2, :], psum[:, u % 2, :], ACT.Copy, scale=out_norm[:, 0:1]).then_inc(mix_t_ready, 1)

                load_table(ACT.Sqrt)
                staggered(act_e, GROUPS, BACK, [(5, keep_mix_t), (3, square_mix), (0, root_back)])
                end_stage(act_e, stage + 3)

            def attention():
                def root_variance(i, u):
                    if u == 0:
                        act_e.wait_ge(a_stats, i + CHUNK_TILES)
                        wait(act_e, a_rstd, i)
                        act_e.activation(std[:, :, :], mean_var[:, :, :, 1], ACT.Sqrt, bias=eps_ln[:, 0:1]).then_inc(a_std, CHUNK_TILES)

                def keep_ln_t(i, u):
                    act_e.wait_ge(a_turned, i + 1)
                    wait(act_e, qkv_done, i - 7)
                    k = u % QUAD
                    act_e.activation(ln_t[:, u // QUAD, k * P:(k + 1) * P], psum[:, 0, 0:P], ACT.Copy).then_inc(a_ln_t, 1)

                def normalise(i, u):
                    q, k = u // QUAD, u % QUAD
                    act_e.wait_ge(a_shift, i - u + CHUNK_TILES)
                    wait(act_e, a_turned, i - 7)
                    act_e.activation(ln[:, q, k, :], x[:, bass.ds(i, 1), :].rearrange("p a m -> p (a m)"),
                                     ACT.Identity, scale=rstd[:, q, k:k + 1], bias=shift[:, q, k:k + 1]).then_inc(a_normed, 1)

                def elu_parts(i, u):
                    act_e.wait_ge(qkv_done, i + 1)
                    wait(act_e, phi_ready, i - 1)
                    act_e.activation(exps[:, u % 2, :], psum[:, 1, 0:2 * P], ACT.Exp)
                    act_e.activation(relus[:, u % 2, :], psum[:, 1, 0:2 * P], ACT.Relu)
                    wait(act_e, state_done, i - 3)
                    wait(act_e, kv_ready, i - 3)
                    act_e.activation(v_one[:, u % 4, :].rearrange("p (h e) -> p h e", h=HEADS)[:, :, 0:HD],
                                     psum[:, 1, 2 * P:3 * P].rearrange("p (h d) -> p h d", h=HEADS), ACT.Copy).then_inc(a_exps, 1)

                def keep_q_t(i, u):
                    act_e.wait_ge(q_turned, i + 1)
                    wait(act_e, inter_done, i - 3)
                    act_e.activation(q_t[:, u % 4, :], psum[:, 6, 0:P], ACT.Copy).then_inc(q_t_ready, 1)

                def keep_att_t(i, u):
                    act_e.wait_ge(att_turned, i + 1)
                    wait(act_e, o_done, i - 1)
                    act_e.activation(att_t[:, u % 2, :], psum[:, 6, 0:P], ACT.Copy).then_inc(att_t_ready, 1)

                load_table(ACT.Sqrt)
                staggered(act_e, TILES, CHUNK_TILES, [(15, keep_q_t), (12, elu_parts), (20, keep_att_t), (10, keep_ln_t),
                                                      (9, normalise), (8, root_variance)])
                end_stage(act_e, 6)

            ffn(0, 2)
            attention()
            ffn(1, 7)

        @block.gpsimd
        def _(pool):
            pool.memset(slot_out[:, :, :], 0.0)
            end_stage(pool, 1)

            def ffn(layer, stage):
                off = layer * GROUPS

                def normalise(i, u):
                    pool.wait_ge(rstd_done, off + i + 1)
                    wait(pool, ln_turned, off + i - 1)
                    pool.tensor_tensor(ln[:, u, :, :], x[:, bass.ds(i * QUAD, QUAD), :],
                                       mean_var[:, u, :, 0:1].broadcast_to([P, QUAD, P]), ALU.subtract).then_inc(centred, 1)
                    pool.wait_ge(centred, off + i + 1)
                    pool.tensor_tensor(ln[:, u, :, :], ln[:, u, :, :],
                                       rstd[:, u, :].unsqueeze(2).broadcast_to([P, QUAD, P]), ALU.mult).then_inc(normed, 1)

                staggered(pool, GROUPS, 2, [(1, normalise)])
                end_stage(pool, stage)

                def hot_rows(j, u):
                    pool.wait_ge(hot_marked, layer * PAIR_QUADS + j + 1)
                    pool.tensor_tensor(hot_row[:, 4 * u:4 * u + 3, :], hot_tile[:, u, :, :],
                                       pair_row[:, bass.ds(j * 4, 3)].unsqueeze(2).broadcast_to([P, 3, SLOT_TILES]),
                                       ALU.mult).then_inc(pool_rows, 1)

                pool.wait_ge(route_pe, 2 * layer + 2)
                staggered(pool, PAIR_QUADS, 2, [(0, hot_rows)])
                end_stage(pool, stage + 1)
                n0 = layer * SLOT_TILES

                def gather(i, u):
                    wait(pool, slot_turned, n0 + i - 3)
                    pool.tensor_copy(gather_now[:, u:u + 1], gather_row[:, bass.ds(i, 1)]).then_inc(gather_indexed, 1)
                    wait_apart(pool, gather_indexed, n0 + i + 1, passed)
                    pool.indirect_dma_start(out=slot_h[:, u, :], out_offset=None, in_=h_dram[:, :],
                                            in_offset=bass.IndirectOffsetOnAxis(ap=gather_now[:, u:u + 1], axis=0)
                                            ).then_inc(gathered[u], 16)

                def scatter(i, u):
                    pool.wait_ge(slot_ready, n0 + i + 1)
                    pool.tensor_copy(scatter_now[:, u:u + 1], scatter_row[:, bass.ds(i, 1)]).then_inc(scatter_indexed, 1)
                    wait_apart(pool, scatter_indexed, n0 + i + 1, passed)
                    pool.indirect_dma_start(out=out_dram[:, :],
                                            out_offset=bass.IndirectOffsetOnAxis(ap=scatter_now[:, u:u + 1], axis=0),
                                            in_=slot_out[:, u, :], in_offset=None).then_inc(scattered[u], 16)

                staggered(pool, SLOT_TILES, 4, [(0, gather), (SCATTER_LAG, scatter)])
                for u in range(4):
                    pool.wait_ge(scattered[u], 4 * (n0 + SLOT_TILES))
                end_stage(pool, stage + 2)

                def scale_first(i, u):
                    pool.wait_ge(back_step, 2 * (off + i) + 2)
                    wait(pool, mixed, off + i - 1)
                    pool.tensor_tensor(scaled_first[:, u % 2, :, :], back[:, u, 0, :, 0:P],
                                       back_scale[:, u % 2, 0, :].unsqueeze(2).broadcast_to([P, QUAD, P]), ALU.mult).then_inc(first_scaled, 1)

                staggered(pool, GROUPS, BACK, [(1, scale_first)])
                end_stage(pool, stage + 3)

            def attention():
                def products(i, u):
                    pool.wait_ge(phi_ready, i + 1)
                    wait(pool, sums_done, 3 * i - 3)
                    k = phi[:, u % 4, P:2 * P].rearrange("p (h d) -> p h d", h=HEADS)
                    v = v_one[:, u % 4, :].rearrange("p (h e) -> p h e", h=HEADS)
                    pool.tensor_tensor(kv[:, u % 2, :].rearrange("p (h e d) -> p h e d", h=HEADS, e=HV),
                                       k.unsqueeze(2).broadcast_to([P, HEADS, HV, HD]),
                                       v.unsqueeze(3).broadcast_to([P, HEADS, HV, HD]), ALU.mult).then_inc(kv_ready, 1)

                def add_bo(i, u):
                    pool.wait_ge(a_normed, i + 1)
                    xt = x[:, bass.ds(i, 1), :].rearrange("p a m -> p (a m)")
                    pool.tensor_tensor(xt, xt, bo[:, :], ALU.add).then_inc(bo_added, 1)

                def halve(i, u):
                    pool.wait_ge(read_done, 3 * i + 3)
                    pairs = read[:, u % 2, :].rearrange("p (n d) -> p n d", d=HD)
                    pool.tensor_tensor(pairs[:, :, 0:HD // 2], pairs[:, :, 0:HD // 2], pairs[:, :, HD // 2:HD], ALU.add).then_inc(halved, 1)

                staggered(pool, TILES, CHUNK_TILES, [(17, halve), (14, products), (14, add_bo)])
                end_stage(pool, 6)

            ffn(0, 2)
            attention()
            ffn(1, 7)

        @block.vector
        def _(dve):
            step = [0]
            dve.memset(ones[:, :], 1.0)
            dve.memset(v_one[:, :, :], 1.0)
            dve.memset(state[:, :, :], 0.0)
            dve.memset(tile_expert[:, :], 0)
            dve.memset(eps_ln[:, :], LN_EPS)
            dve.memset(eps_rms[:, :], RMS_EPS).then_inc(ones_set, 1)
            dve.wait_ge(early_loaded, 16 * len(EARLY_LOADS))
            end_stage(dve, 1)

            def split_bias():
                made = [0]

                def parts(instruction):
                    made[0] += 1
                    instruction.then_inc(parts_made, 1)
                    dve.wait_ge(parts_made, made[0])

                parts(dve.memset(kv[:, 0, 4 * P:5 * P], 0.0))
                for p in (0, 32, 64):
                    last = dve.memset(kv[p:p + 1, 0, 4 * P:5 * P], 1.0)
                parts(last)
                parts(dve.tensor_copy(part_ones[:, :], kv[:, 0, 4 * P:5 * P]))
                parts(dve.tensor_copy(bias_parts[:, :], bqkv))
                parts(dve.tensor_tensor(bias_rest, bqkv, bias_parts[:, :], ALU.subtract))
                parts(dve.tensor_copy(bias_parts[32:64, :], kv[32:64, 1, 0:3 * P]))
                parts(dve.tensor_copy(bias_parts[64:96, :], kv[64:96, 1, 0:3 * P]))
                parts(dve.tensor_tensor(kv[64:96, 1, 0:3 * P], kv[64:96, 1, 0:3 * P], bias_parts[64:96, :], ALU.subtract))
                parts(dve.tensor_copy(bias_parts[64:96, :], kv[64:96, 1, 0:3 * P]))


            def ffn(layer, stage):
                off = layer * GROUPS

                def statistics(i, u):
                    if layer == 0 and isinstance(i, int) and i in X_PIECES:
                        dve.wait_ge(x_loaded[X_PIECES.index(i)], 16)
                    wait(dve, normed, off + i - 1)
                    for k in range(QUAD):
                        last = dve.bn_stats(stats[:, u, k, :], x[:, bass.ds(i * QUAD + k, 1), :].rearrange("p a m -> p (a m)"))
                    last.then_inc(bn_done, 1)
                    wait_apart(dve, bn_done, off + i + 1, passed)
                    for k in range(QUAD):
                        last = dve.bn_aggr(mean_var[:, u, k, :], stats[:, u, k, :])
                    last.then_inc(stats_done, 1)

                def reciprocals(i, u):
                    dve.wait_ge(std_ready, off + i + 1)
                    wait(dve, normed, off + i - 1)
                    dve.reciprocal(rstd[:, u, :], std[:, u, :]).then_inc(rstd_done, 1)

                def scale_h(i, u):
                    dve.wait_ge(rms_ready, off + i + 1)
                    dve.reciprocal(rrms[:, u, :], rms[:, u, :]).then_inc(rrms_done, 1)
                    wait(dve, h_turned, off + i - 1)
                    wait(dve, h_stored[u], 8 * (off + i) - 8 * u)
                    dve.wait_ge(rrms_done, off + i + 1)
                    dve.tensor_tensor(h[:, u, :, :], psum[:, 2 + u, :].rearrange("p (k m) -> p k m", m=P),
                                      rrms[:, u, :].unsqueeze(2).broadcast_to([P, QUAD, P]), ALU.mult).then_inc(h_scaled, 1)

                def keep_logits(i, u):
                    dve.wait_ge(logits_done, off + i + 1)
                    dve.tensor_copy(logits[:, bass.ds(i * QUAD, QUAD), :].rearrange("p k e -> p (k e)"),
                                    psum[:, 6 + u, 0:QUAD * EXPERTS]).then_inc(logits_kept, 1)

                staggered(dve, GROUPS, 2, [(5, scale_h), (1, reciprocals), (0, statistics), (8, keep_logits)])
                if layer == 0:
                    dve.wait_ge(loaded, 16 * N_LATER)
                    dve.tensor_copy(iota_bf[:, :], iota_col[:, :])
                    dve.tensor_scalar(less_row[:, :], pair_row[:, :], -1.0, None, ALU.mult)
                end_stage(dve, stage)


                def then(instruction):
                    step[0] += 1
                    instruction.then_inc(route_step, 1)
                    dve.wait_ge(route_step, step[0])

                def over_experts(ap):
                    return ap.unsqueeze(2).broadcast_to([P, TILES, EXPERTS])

                def over_tiles(ap):
                    return ap.unsqueeze(1).broadcast_to([P, TILES, EXPERTS])

                then(dve.tensor_tensor(scratch[:, :, :], logits[:, :, :], over_tiles(rbias[:, :]), ALU.add))
                diagonal = beats.rearrange("p t a b -> p t (a b)")[:, :, 0:EXPERTS * EXPERTS:EXPERTS + 1]
                then(dve.memset(diagonal, 0.0))
                for e in range(EXPERTS):
                    if e:
                        last = dve.tensor_tensor(beats[:, :, e, 0:e], scratch[:, :, 0:e],
                                                 scratch[:, :, e:e + 1].broadcast_to([P, TILES, e]), ALU.is_ge)
                    if e < EXPERTS - 1:
                        n = EXPERTS - 1 - e
                        last = dve.tensor_tensor(beats[:, :, e, e + 1:EXPERTS], scratch[:, :, e + 1:EXPERTS],
                                                 scratch[:, :, e:e + 1].broadcast_to([P, TILES, n]), ALU.is_gt)
                then(last)
                half = EXPERTS // 2
                while half > 1:
                    then(dve.tensor_tensor(beats[:, :, :, 0:half], beats[:, :, :, 0:half], beats[:, :, :, half:2 * half], ALU.add))
                    half //= 2
                then(dve.tensor_tensor(slot_of[:, :, :], beats[:, :, :, 0], beats[:, :, :, 1], ALU.add))
                then(dve.tensor_scalar(picked[:, :, :], slot_of[:, :, :], float(TOP) - 0.5, None, ALU.is_lt))
                dve.tensor_reduce(picks_here[:, :], picked[:, :, :].rearrange("p t e -> p e t"), AX.X, ALU.add).then_inc(route_pe, 1)
                dve.wait_ge(route_act, 2 * layer + 1)
                then(dve.tensor_copy(counts[:, :], psum[:, 1, 0:EXPERTS]))
                then(dve.tensor_scalar(row_tmp[:, 0:TILES], iota_col[:, 0:TILES], float(P), None, ALU.mult))
                then(dve.tensor_tensor(over, counts[:, :].unsqueeze(2).broadcast_to([P, EXPERTS, TILES]),
                                       row_tmp[:, 0:TILES].unsqueeze(1).broadcast_to([P, EXPERTS, TILES]), ALU.is_gt))
                then(dve.tensor_reduce(tile_count[:, :], over, AX.X, ALU.add))
                then(dve.tensor_tensor_scan(tile_end[:, :], ones[:, 0:EXPERTS], tile_count[:, :], 0.0, ALU.mult, ALU.add))
                then(dve.tensor_tensor(first_slot[:, :], tile_end[:, :], tile_count[:, :], ALU.subtract))
                then(dve.scalar_tensor_tensor(out=first_slot[:, :], in0=first_slot[:, :], scalar=float(P),
                                              in1=psum[:, 0, 0:EXPERTS], op0=ALU.mult, op1=ALU.add))
                for e in range(EXPERTS):
                    last = dve.tensor_tensor_scan(slot_of[:, :, e], ones[:, 0:TILES], picked[:, :, e],
                                                  first_slot[:, e:e + 1], ALU.mult, ALU.add)
                then(last)
                then(dve.tensor_tensor(slot_of[:, :, :], slot_of[:, :, :], picked[:, :, :], ALU.subtract))
                then(dve.tensor_tensor(slot_of[:, :, :], slot_of[:, :, :], picked[:, :, :], ALU.mult))
                then(dve.tensor_reduce(pair_slot[:, 1, :], slot_of[:, :, :], AX.X, ALU.max))
                then(dve.tensor_reduce(per_token[:, 0, :], slot_of[:, :, :], AX.X, ALU.add))
                then(dve.tensor_tensor(pair_slot[:, 0, :], per_token[:, 0, :], pair_slot[:, 1, :], ALU.subtract))
                then(dve.tensor_copy(pair_int[:, 0, :, :], pair_slot[:, :, :]))
                then(dve.tensor_scalar(pair_int[:, 1, :, :], pair_int[:, 0, :, :], P - 1, None, ALU.bitwise_and))
                then(dve.tensor_copy(pair_place[:, :, :], pair_int[:, 1, :, :]))
                then(dve.tensor_tensor(pair_tile[:, :, :], pair_slot[:, :, :], pair_place[:, :, :], ALU.subtract))
                then(dve.tensor_scalar(pair_tile[:, :, :], pair_tile[:, :, :], 1.0 / P, None, ALU.mult))
                then(dve.tensor_tensor(ended, tile_end[:, :].unsqueeze(1).broadcast_to([P, SLOT_TILES, EXPERTS]),
                                       iota_col[:, :].unsqueeze(2).broadcast_to([P, SLOT_TILES, EXPERTS]), ALU.is_le))
                then(dve.tensor_reduce(row_tmp[:, :], ended, AX.X, ALU.add))
                then(dve.tensor_scalar(row_tmp[:, :], row_tmp[:, :], float(EXPERTS - 1), float(P), ALU.min, ALU.mult))
                then(dve.tensor_copy(tile_expert[:, 3:3 + SLOT_TILES], row_tmp[:, :]))
                dve.memset(hot_place[:, 0, :], 0.0)
                dve.memset(hot_row[:, 0, :], 0.0).then_inc(route_pe, 1)
                dve.wait_ge(route_act, 2 * layer + 2)

                slots = pair_place[:, :, :].rearrange("p w t -> p (w t)")
                tiles = pair_tile[:, :, :].rearrange("p w t -> p (w t)")

                def one_hots(j, u):
                    wait(dve, hot_used, layer * PAIR_QUADS + j - 1)
                    for k in range(3):
                        last = dve.tensor_scalar(hot_tile[:, u, k, :], iota_bf[:, :], tiles[:, bass.ds(j * 4 + k, 1)], None, ALU.is_equal)
                    last.then_inc(hot_marked, 1)
                    for k in range(4):
                        last = dve.tensor_scalar(hot_place[:, 4 * u + k, :], iota_bf[:, 0:P], slots[:, bass.ds(j * 4 + k, 1)], None,
                                                 ALU.is_equal)
                    last.then_inc(hot_ready, 1)

                staggered(dve, PAIR_QUADS, 2, [(0, one_hots)])
                dve.wait_ge(hot_used, (layer + 1) * PAIR_QUADS)
                then(dve.tensor_scalar(row_of[:, :], psum[:, 2, 0:SLOT_TILES], -1.0, None, ALU.add))
                then(dve.tensor_scalar(row_tmp[:, :], row_of[:, :], 0.0, None, ALU.is_lt))
                then(dve.tensor_tensor(row_tmp[:, :], row_tmp[:, :], spare_row[:, :], ALU.mult))
                then(dve.tensor_tensor(row_tmp[:, :], row_tmp[:, :], row_of[:, :], ALU.add))
                then(dve.tensor_copy(scatter_row[:, :], row_tmp[:, :]))
                then(dve.tensor_scalar(row_tmp[:, :], row_of[:, :], float(TILES * P), -float(TILES * P), ALU.is_ge, ALU.mult))
                then(dve.tensor_tensor(row_tmp[:, :], row_tmp[:, :], row_of[:, :], ALU.add))
                then(dve.tensor_scalar(row_tmp[:, :], row_tmp[:, :], 0.0, None, ALU.max))
                then(dve.tensor_copy(gather_row[:, :], row_tmp[:, :]))
                end_stage(dve, stage + 1)

                if layer == 0:
                    split_bias()
                n0 = layer * SLOT_TILES
                registers = [dve.alloc_register(f"dve_expert_{layer}_{k}") for k in range(6)]
                norm_at = {}

                def read_experts(t):
                    dve.load(registers, tile_expert[0:1, bass.ds(t + 1, 6)])
                    for k in range(6):
                        norm_at[k] = dve.snap(registers[k], min_val=0, max_val=(EXPERTS - 1) * P)

                def fetch_gate(i, u):
                    if layer == 0 and isinstance(i, int) and i == 0:
                        dve.wait_ge(experts_loaded, 48)
                    wait(dve, gate_up, n0 + i - 1)
                    dve.tensor_copy(gate_now[:, u % 2, :], wg[:, bass.ds(norm_at[u + 2] * CHUNKS, FF)]).then_inc(gate_fetched, 1)

                def times_up(i, u):
                    dve.wait_ge(silu_done, n0 + i + 1)
                    wait(dve, down_done, n0 + i - 1)
                    dve.tensor_tensor(act_t[:, u % 2, :], silu[:, u % 2, :], psum[:, 3 + u % 2, :], ALU.mult).then_inc(act_done, 1)

                def scale_slots(i, u):
                    dve.wait_ge(slot_sumsq, n0 + i + 1)
                    at = norm_at[(u + 2) % 4]
                    dve.tensor_tensor(slot_out[:, u, 0:P], psum[:, 5 + u % 2, 0:P], enorm[:, bass.ds(at, P)], ALU.mult).then_inc(slot_ready, 1)

                staggered(dve, SLOT_TILES, 4, [(0, fetch_gate), (1, times_up), (2, scale_slots)], before=read_experts)

                then(dve.tensor_scalar(scratch[:, :, :], picked[:, :, :], -1.0, 1e30, ALU.add, ALU.mult))
                then(dve.tensor_tensor(scratch[:, :, :], scratch[:, :, :], logits[:, :, :], ALU.add))
                then(dve.tensor_reduce(per_token[:, 0, :], scratch[:, :, :], AX.X, ALU.max))
                dve.tensor_tensor(scratch[:, :, :], scratch[:, :, :], over_experts(per_token[:, 0, :]),
                                  ALU.subtract).then_inc(route_exp, 1)
                dve.wait_ge(route_exp, 2 * layer + 2)
                then(dve.tensor_reduce(per_token[:, 0, :], gates[:, :, :], AX.X, ALU.add))
                then(dve.reciprocal(per_token[:, 1, :], per_token[:, 0, :]))
                then(dve.tensor_tensor(gates[:, :, :], gates[:, :, :], over_experts(per_token[:, 1, :]), ALU.mult))
                end_stage(dve, stage + 2)

                then(dve.tensor_tensor(scratch[:, :, :], slot_of[:, :, :], over_experts(pair_slot[:, 1, :]), ALU.is_equal))
                then(dve.tensor_tensor(scratch[:, :, :], scratch[:, :, :], gates[:, :, :], ALU.mult))
                then(dve.tensor_reduce(pair_gate[:, 1, :], scratch[:, :, :], AX.X, ALU.add))
                then(dve.tensor_tensor(scratch[:, :, :], gates[:, :, :], scratch[:, :, :], ALU.subtract))
                then(dve.tensor_reduce(pair_gate[:, 0, :], scratch[:, :, :], AX.X, ALU.add))

                def scales(i, u):
                    dve.wait_ge(back_rms_ready, off + i + 1)
                    wait(dve, mixed, off + i - 1)
                    dve.reciprocal(back_scale[:, u % 2, :, :], back_rms[:, u % 2, :, :]).then_inc(back_step, 1)
                    dve.wait_ge(back_step, 2 * (off + i) + 1)
                    dve.tensor_tensor(back_scale[:, u % 2, :, :], back_scale[:, u % 2, :, :],
                                      pair_gate[:, :, bass.ds(i * QUAD, QUAD)], ALU.mult).then_inc(back_step, 1)

                def mix(i, u):
                    dve.wait_ge(first_scaled, off + i + 1)
                    wait(dve, mix_scaled, off + i - 1)
                    wait(dve, mix_sumsq, off + i - 1)
                    for k in range(QUAD):
                        last = dve.scalar_tensor_tensor(out=ln[:, u % 2, k, :], in0=back[:, u, 1, k, 0:P],
                                                        scalar=back_scale[:, u % 2, 1, k:k + 1], in1=scaled_first[:, u % 2, k, :],
                                                        op0=ALU.mult, op1=ALU.add)
                    last.then_inc(mixed, 1)

                def scale_mix(i, u):
                    dve.wait_ge(mix_rms_ready, off + i + 1)
                    dve.reciprocal(rrms[:, u % 2, :], rms[:, u % 2, :]).then_inc(mix_rrms, 1)
                    wait(dve, mix_turned, off + i - 1)
                    dve.wait_ge(mix_rrms, off + i + 1)
                    dve.tensor_tensor(h[:, u % 2, :, :], ln[:, u % 2, :, :],
                                      rrms[:, u % 2, :].unsqueeze(2).broadcast_to([P, QUAD, P]), ALU.mult).then_inc(mix_scaled, 1)

                def add_x(i, u):
                    dve.wait_ge(y_done, off + i + 1)
                    xs = x[:, bass.ds(i * QUAD, QUAD), :].rearrange("p k m -> p (k m)")
                    dve.scalar_tensor_tensor(out=xs, in0=psum[:, 2 + u % 2, :], scalar=0.5, in1=xs, op0=ALU.mult,
                                             op1=ALU.add).then_inc(x_added, 1)

                staggered(dve, GROUPS, BACK, [(4, scale_mix), (2, mix), (7, add_x), (1, scales)])
                end_stage(dve, stage + 3)

            def attention():
                def statistics(i, u):
                    wait(dve, a_stats, i - 7)
                    dve.bn_stats(stats[:, u // QUAD, u % QUAD, :], x[:, bass.ds(i, 1), :].rearrange("p a m -> p (a m)")).then_inc(a_bn, 1)

                def aggregate(i, u):
                    wait_apart(dve, a_bn, i + 1, passed)
                    if u == 0 and not (isinstance(i, int) and i == 0):
                        wait_apart(dve, a_shift, i, passed)
                    dve.bn_aggr(mean_var[:, u // QUAD, u % QUAD, :], stats[:, u // QUAD, u % QUAD, :]).then_inc(a_stats, 1)

                def reciprocals(i, u):
                    if u == 0:
                        dve.wait_ge(a_std, i + CHUNK_TILES)
                        wait(dve, a_normed, i)
                        dve.reciprocal(rstd[:, :, :], std[:, :, :]).then_inc(a_rstd, CHUNK_TILES)
                        dve.wait_ge(a_rstd, i + CHUNK_TILES)
                        dve.scalar_tensor_tensor(out=shift[:, :, :], in0=mean_var[:, :, :, 0], scalar=-1.0, in1=rstd[:, :, :],
                                                 op0=ALU.mult, op1=ALU.mult).then_inc(a_shift, CHUNK_TILES)

                def make_phi(i, u):
                    dve.wait_ge(a_exps, i + 1)
                    wait(dve, state_done, i - 3)
                    wait(dve, kv_ready, i - 3)
                    dve.scalar_tensor_tensor(out=phi[:, u % 4, :], in0=exps[:, u % 2, :], scalar=1.0, in1=relus[:, u % 2, :],
                                             op0=ALU.min, op1=ALU.add).then_inc(phi_ready, 1)

                def keep_state(i, u):
                    dve.wait_ge(state_done, i + 1)
                    wait(dve, inter_done, i - 2)
                    if u == CHUNK_TILES - 1:
                        dve.memset(state[:, u % 4, :], 0.0).then_inc(state_ready, 1)
                        return
                    dve.tensor_tensor(state[:, u % 4, :], psum[:, 5, 0:HEADS * HV], head_mask[:, :], ALU.mult).then_inc(state_ready, 1)

                def read_sums(i, u):
                    q = phi[:, u % 4, 0:P].rearrange("p (h d) -> p h d", h=HEADS)
                    wait(dve, reduced, i - 1)
                    for n, (a, b) in enumerate(THIRDS):
                        h0, h1 = a // (HV * HD), b // (HV * HD)
                        dve.wait_ge(sums_done, 3 * i + n + 1)
                        dve.tensor_tensor(read[:, u % 2, a:b].rearrange("p (h e d) -> p h e d", e=HV, d=HD),
                                          psum[:, 2 + n, 0:b - a].rearrange("p (h e d) -> p h e d", e=HV, d=HD),
                                          q[:, h0:h1, :].unsqueeze(2).broadcast_to([P, h1 - h0, HV, HD]), ALU.mult).then_inc(read_done, 1)

                def reduce_sums(i, u):
                    dve.wait_ge(halved, i + 1)
                    wait(dve, att_ready, i - 1)
                    dve.tensor_reduce(intra[:, u % 2, :], read[:, u % 2, :].rearrange("p (n d) -> p n d", d=HD)[:, :, 0:HD // 2],
                                      AX.X, ALU.add).then_inc(reduced, 1)

                def add_inter(i, u):
                    dve.wait_ge(reduced, i + 1)
                    dve.wait_ge(inter_done, i + 1)
                    dve.tensor_tensor(intra[:, u % 2, :], intra[:, u % 2, :], psum[:, 7, 0:HEADS * HV], ALU.add).then_inc(total_done, 1)

                def invert(i, u):
                    dve.wait_ge(total_done, i + 1)
                    both = intra[:, u % 2, :].rearrange("p (h e) -> p h e", h=HEADS)
                    dve.reciprocal(recip_den[:, u % 2, :], both[:, :, HD]).then_inc(den_done, 1)

                def divide(i, u):
                    both = intra[:, u % 2, :].rearrange("p (h e) -> p h e", h=HEADS)
                    dve.wait_ge(den_done, i + 1)
                    wait(dve, att_turned, i - 1)
                    dve.tensor_tensor(att[:, u % 2, :].rearrange("p (h d) -> p h d", h=HEADS), both[:, :, 0:HD],
                                      recip_den[:, u % 2, :].unsqueeze(2).broadcast_to([P, HEADS, HD]), ALU.mult).then_inc(att_ready, 1)

                def add_x(i, u):
                    dve.wait_ge(o_done, i + 1)
                    dve.wait_ge(bo_added, i + 1)
                    xt = x[:, bass.ds(i, 1), :].rearrange("p a m -> p (a m)")
                    dve.tensor_tensor(xt, psum[:, 0, 0:P], xt, ALU.add).then_inc(att_added, 1)

                staggered(dve, TILES, CHUNK_TILES, [(18, reduce_sums), (0, statistics), (16, read_sums), (19, add_inter),
                                                    (16, keep_state), (19, invert), (13, make_phi), (22, add_x), (19, divide),
                                                    (9, reciprocals), (1, aggregate)])
                end_stage(dve, 6)

            ffn(0, 2)
            attention()
            ffn(1, 7)


def kernel(L0_attn_x, L0_attn_Wq, L0_attn_bq, L0_attn_Wk, L0_attn_bk, L0_attn_Wv, L0_attn_bv, L0_attn_Wo, L0_attn_bo,
           L0_ffn_W_in, L0_ffn_in_norm_w, L0_ffn_Wr, L0_ffn_expert_bias, L0_ffn_Wg, L0_ffn_Wu, L0_ffn_Wd,
           L0_ffn_enorm_w, L0_ffn_out_norm_w, L0_ffn_W_out):
    import concourse.bacc as bacc
    from concourse.bass_utils import run_bass_kernel_spmd

    def laid(a):
        return np.ascontiguousarray(a)

    part, col = np.arange(P)[:, None], np.arange(P)[None, :]
    tiles = np.arange(SLOT_TILES)[None, :]
    head = np.arange(HEADS * HV)[None, :] // HV
    arrays = {
        "x": laid(np.reshape(L0_attn_x, (BATCH * SEQ, P))),
        "w_in": laid(np.transpose(L0_ffn_W_in)), "w_out": laid(np.transpose(L0_ffn_W_out)),
        "wo": laid(np.transpose(L0_attn_Wo)), "wr": laid(np.transpose(L0_ffn_Wr)),
        "wqkv": laid(np.concatenate([np.transpose(L0_attn_Wq), np.transpose(L0_attn_Wk), np.transpose(L0_attn_Wv)], 1)),
        "wg": laid(np.transpose(L0_ffn_Wg, (2, 0, 1)).reshape(P, EXPERTS * FF)),
        "wu": laid(np.transpose(L0_ffn_Wu, (2, 0, 1)).reshape(P, EXPERTS * FF)),
        "wd": laid(np.transpose(np.reshape(L0_ffn_Wd, (EXPERTS, P, CHUNKS, P)), (3, 0, 2, 1)).reshape(P, EXPERTS * FF)),
        "in_norm": laid(np.reshape(L0_ffn_in_norm_w, (P, 1))), "out_norm": laid(np.reshape(L0_ffn_out_norm_w, (P, 1))),
        "enorm": laid(np.reshape(L0_ffn_enorm_w, (EXPERTS * P,))), "rbias": laid(L0_ffn_expert_bias),
        "bqkv": laid(np.concatenate([L0_attn_bq, L0_attn_bk, L0_attn_bv])), "bo": laid(L0_attn_bo),
        "ident": laid((part == col).astype(np.float32)),
        "upto_here": laid((part <= col).astype(np.float32)),
        "before_here": laid((part < col).astype(np.float32)),
        "head_mask": laid((part // HD == head).astype(np.float32)),
        "iota_col": laid(np.broadcast_to(tiles, (P, SLOT_TILES)).astype(np.float32)),
        "pair_row": laid((1 + P * np.arange(TOP * TILES)[None, :] + part).astype(np.float32)),
        "spare_row": laid((OUT_ROWS + 1 + P * tiles + part).astype(np.float32)),
    }
    nc = bacc.Bacc("TRN2", target_bir_lowering=False, num_devices=1)
    d = {n: nc.dram_tensor("in_" + n, a.shape, F32, kind="ExternalInput").ap() for n, a in arrays.items()}
    d["out"] = nc.dram_tensor("out_x", (BATCH * SEQ, P), F32, kind="ExternalOutput").ap()
    build(nc, d)
    r = run_bass_kernel_spmd(nc, [{"in_" + n: a for n, a in arrays.items()}], core_ids=[0])
    return r.results[0]["out_x"].reshape(BATCH, SEQ, P)
```
